# Optimizing a Trainium2 kernel written in Bass

```python
import numpy as np
import jax
import jax.numpy as jnp

def _softmax(x, axis=-1):
    return jax.nn.softmax(x, axis=axis)

def _gelu(x):
    return jax.nn.gelu(x, approximate=True)

def _silu(x):
    return jax.nn.silu(x)

def _sigmoid(x):
    return jax.nn.sigmoid(x)

def _layernorm(x, axis=-1, eps=1e-05):
    m = jnp.mean(x, axis=axis, keepdims=True)
    v = jnp.var(x, axis=axis, keepdims=True)
    return (x - m) / jnp.sqrt(v + eps)

def _scatter_add(tgt, idx, src, axis=0):
    return tgt.at[idx].add(src)

def _segment_sum(src, seg, n):
    return jax.ops.segment_sum(src, seg, n)
kernel_name = 'mk_seq_postln_d1_jaxref_r4_981e43'

def setup_inputs(seed: int=0):
    np.random.seed(seed)
    _w = jnp.asarray

    def _L0_attn_setup():
        import jax, jax.numpy as jnp
        import numpy as np
        import math
        N_HEAD = 16

        def _causal_attn(q, k, v):
            d_k = q.shape[-1]
            s = jnp.einsum('bhqd,bhkd->bhqk', q, k) / math.sqrt(d_k)
            L, S = (q.shape[-2], k.shape[-2])
            mask = jnp.tril(jnp.ones((L, S), dtype=bool))
            s = jnp.where(mask, s, -jnp.inf)
            a = jax.nn.softmax(s, axis=-1)
            return jnp.einsum('bhqk,bhkd->bhqd', a, v)
        key = jax.random.key(seed)
        ks = jax.random.split(key, 8)
        B, T, C = (2, 512, 256)
        scale = 0.02
        return {'x': jax.random.normal(ks[0], (B, T, C), dtype=jnp.float32), 'W_attn': jax.random.normal(ks[1], (C, 2 * C), dtype=jnp.float32) * scale, 'b_attn': jnp.zeros((2 * C,), dtype=jnp.float32), 'W_k2': jax.random.normal(ks[2], (C, C), dtype=jnp.float32) * scale, 'b_k2': jnp.zeros((C,), dtype=jnp.float32), 'W_proj': jax.random.normal(ks[3], (C, C), dtype=jnp.float32) * scale, 'b_proj': jnp.zeros((C,), dtype=jnp.float32)}
    _L0_attn_in = _L0_attn_setup()

    def _L0_ffn_setup():
        import jax, jax.numpy as jnp
        import numpy as np
        NUM_EXPERTS = 8
        HIDDEN = 256
        INTER = 256
        BATCH = 2
        SEQ = 256
        TOP_K = 2
        SWIGLU_ALPHA = 1.702
        LIMIT = 7.0

        def _grouped_mm(x, w, expert_ids):
            onehot = jax.nn.one_hot(expert_ids, w.shape[0], dtype=x.dtype)
            y_all = jnp.einsum('tk,ekn->etn', x, w)
            return jnp.einsum('te,etn->tn', onehot, y_all)

        def _gpt_oss_swiglu(x):
            gate = jnp.minimum(x[..., ::2], LIMIT)
            up = jnp.clip(x[..., 1::2], -LIMIT, LIMIT)
            glu = gate * jax.nn.sigmoid(gate * SWIGLU_ALPHA)
            return (up + 1.0) * glu
        key = jax.random.key(seed)
        ks = jax.random.split(key, 7)
        hidden_states = jax.random.normal(ks[0], (BATCH, SEQ, HIDDEN), jnp.float32)
        router_indices = jax.random.randint(ks[1], (BATCH * SEQ, TOP_K), 0, NUM_EXPERTS)
        routing_weights = jax.nn.softmax(jax.random.normal(ks[2], (BATCH * SEQ, NUM_EXPERTS), jnp.float32), axis=-1)
        scale = 0.02
        gate_up_proj = jax.random.normal(ks[3], (NUM_EXPERTS, HIDDEN, 2 * INTER), jnp.float32) * scale
        gate_up_proj_bias = jax.random.normal(ks[4], (NUM_EXPERTS, 2 * INTER), jnp.float32) * scale
        down_proj = jax.random.normal(ks[5], (NUM_EXPERTS, INTER, HIDDEN), jnp.float32) * scale
        down_proj_bias = jax.random.normal(ks[6], (NUM_EXPERTS, HIDDEN), jnp.float32) * scale
        return {'hidden_states': hidden_states, 'router_indices': router_indices, 'routing_weights': routing_weights, 'gate_up_proj': gate_up_proj, 'gate_up_proj_bias': gate_up_proj_bias, 'down_proj': down_proj, 'down_proj_bias': down_proj_bias}
    _L0_ffn_in = _L0_ffn_setup()
    _d = {'L0_attn_x': _L0_attn_in['x'], 'L0_attn_W_attn': _L0_attn_in['W_attn'], 'L0_attn_b_attn': _L0_attn_in['b_attn'], 'L0_attn_W_k2': _L0_attn_in['W_k2'], 'L0_attn_b_k2': _L0_attn_in['b_k2'], 'L0_attn_W_proj': _L0_attn_in['W_proj'], 'L0_attn_b_proj': _L0_attn_in['b_proj'], 'L0_ffn_router_indices': _L0_ffn_in['router_indices'], 'L0_ffn_routing_weights': _L0_ffn_in['routing_weights'], 'L0_ffn_gate_up_proj': _L0_ffn_in['gate_up_proj'], 'L0_ffn_gate_up_proj_bias': _L0_ffn_in['gate_up_proj_bias'], 'L0_ffn_down_proj': _L0_ffn_in['down_proj'], 'L0_ffn_down_proj_bias': _L0_ffn_in['down_proj_bias']}
    _x0 = _d['L0_attn_x']
    _d['L0_attn_x'] = jax.random.normal(jax.random.fold_in(jax.random.key(seed), 1), (32, 512, 256), dtype=_x0.dtype)
    del _x0
    return _d

def reference(L0_attn_x, L0_attn_W_attn, L0_attn_b_attn, L0_attn_W_k2, L0_attn_b_k2, L0_attn_W_proj, L0_attn_b_proj, L0_ffn_router_indices, L0_ffn_routing_weights, L0_ffn_gate_up_proj, L0_ffn_gate_up_proj_bias, L0_ffn_down_proj, L0_ffn_down_proj_bias):

    def _L0_attn_ref(x, W_attn, b_attn, W_k2, b_k2, W_proj, b_proj):
        import jax, jax.numpy as jnp
        import numpy as np
        import math
        N_HEAD = 16

        def _causal_attn(q, k, v):
            d_k = q.shape[-1]
            s = jnp.einsum('bhqd,bhkd->bhqk', q, k) / math.sqrt(d_k)
            L, S = (q.shape[-2], k.shape[-2])
            mask = jnp.tril(jnp.ones((L, S), dtype=bool))
            s = jnp.where(mask, s, -jnp.inf)
            a = jax.nn.softmax(s, axis=-1)
            return jnp.einsum('bhqk,bhkd->bhqd', a, v)
        B, T, C = x.shape
        H = N_HEAD
        d = C // H
        qk = x @ W_attn + b_attn
        q, k = (qk[..., :C], qk[..., C:])
        q = q.reshape(B, T, H, d).transpose(0, 2, 1, 3)
        k = k.reshape(B, T, H, d).transpose(0, 2, 1, 3)
        v = x.reshape(B, T, H, d).transpose(0, 2, 1, 3)
        y = _causal_attn(q, k, v)
        e = v[:, :, 1:, :] - y[:, :, :-1, :]
        k2 = (x[:, :-1] @ W_k2 + b_k2).reshape(B, T - 1, H, d).transpose(0, 2, 1, 3)
        q2 = q[:, :, 1:, :]
        y2 = _causal_attn(q2, k2, e)
        y2 = jnp.concatenate([jnp.zeros_like(y2[:, :, :1, :]), y2], axis=2)

        def proj(t):
            return t.transpose(0, 2, 1, 3).reshape(B, T, C) @ W_proj + b_proj
        return proj(y) + proj(y2)

    def _L0_ffn_ref(hidden_states, router_indices, routing_weights, gate_up_proj, gate_up_proj_bias, down_proj, down_proj_bias):
        import jax, jax.numpy as jnp
        import numpy as np
        NUM_EXPERTS = 8
        HIDDEN = 256
        INTER = 256
        BATCH = 2
        SEQ = 256
        TOP_K = 2
        SWIGLU_ALPHA = 1.702
        LIMIT = 7.0

        def _grouped_mm(x, w, expert_ids):
            onehot = jax.nn.one_hot(expert_ids, w.shape[0], dtype=x.dtype)
            y_all = jnp.einsum('tk,ekn->etn', x, w)
            return jnp.einsum('te,etn->tn', onehot, y_all)

        def _gpt_oss_swiglu(x):
            gate = jnp.minimum(x[..., ::2], LIMIT)
            up = jnp.clip(x[..., 1::2], -LIMIT, LIMIT)
            glu = gate * jax.nn.sigmoid(gate * SWIGLU_ALPHA)
            return (up + 1.0) * glu
        B = hidden_states.shape[0]
        H = hidden_states.shape[-1]
        x = hidden_states.reshape(-1, H)
        M = x.shape[0]
        top_k = router_indices.shape[1]
        num_experts = gate_up_proj.shape[0]
        topk_weights = jnp.take_along_axis(routing_weights, router_indices, axis=1)
        flat_experts = router_indices.reshape(-1)
        sort_idx = jnp.argsort(flat_experts)
        sorted_pos = sort_idx // top_k
        expert_sorted = flat_experts[sort_idx]
        grouped = x[sorted_pos]
        gate_up = _grouped_mm(grouped, gate_up_proj, expert_sorted)
        gate_up = gate_up + gate_up_proj_bias[expert_sorted]
        inter = _gpt_oss_swiglu(gate_up)
        down = _grouped_mm(inter, down_proj, expert_sorted)
        down = down + down_proj_bias[expert_sorted]
        down = down * topk_weights.reshape(-1)[sort_idx][:, None]
        out = jnp.zeros((M, H), x.dtype).at[sorted_pos].add(down)
        return out.reshape(B, -1, H)
    x = L0_attn_x
    x = _layernorm(x + _L0_attn_ref(x, L0_attn_W_attn, L0_attn_b_attn, L0_attn_W_k2, L0_attn_b_k2, L0_attn_W_proj, L0_attn_b_proj), axis=-1)
    x = _layernorm(x + _L0_ffn_ref(x, L0_ffn_router_indices, L0_ffn_routing_weights, L0_ffn_gate_up_proj, L0_ffn_gate_up_proj_bias, L0_ffn_down_proj, L0_ffn_down_proj_bias), axis=-1)
    return x

_drawn_inputs = setup_inputs


def setup_inputs(seed=0):
    import zlib

    import numpy as np

    out = dict(_drawn_inputs(seed))
    spreads = {'L0_attn_b_attn': (0.0, 0.8), 'L0_attn_b_k2': (0.0, 2.0), 'L0_attn_b_proj': (0.0, 0.1)}
    factors = {'L0_attn_W_attn': 8.0,
     'L0_attn_W_k2': 8.0,
     'L0_ffn_routing_weights': 8.0,
     'L0_ffn_gate_up_proj': 8.0,
     'L0_ffn_gate_up_proj_bias': 29.498,
     'L0_ffn_down_proj': 8.0,
     'L0_ffn_down_proj_bias': 200.0}
    for name, (base, spread) in spreads.items():
        noise = np.random.default_rng([zlib.crc32(name.encode()), seed]).standard_normal(out[name].shape)
        drawn = base * np.exp(spread * noise) if base else spread * noise
        out[name] = jnp.asarray(drawn.astype(out[name].dtype))
    for name, factor in factors.items():
        out[name] = (out[name] * factor).astype(out[name].dtype)
    return out
```

```python
from contextlib import ExitStack

import numpy as np

import concourse.bass as bass
from concourse import mybir

F32 = mybir.dt.float32
BF16 = mybir.dt.bfloat16
I32 = mybir.dt.int32
ALU = mybir.AluOpType
ACT = mybir.ActivationFunctionType

P = 128
HEADS, HEAD_DIM = 16, 16
GROUP = 4
GROUPS = HEADS // GROUP
UNITS = 2 * GROUPS
SLOTS = 5
LEAD = 6
PARTS_Q = (0, 0, 1, 0, 2, 1)
PARTS_K = (0, 1, 0, 2, 0, 1)
TERMS = len(PARTS_Q)
SCORE_ROWS = TERMS * HEAD_DIM
MAX_PARTS = 3
MASKED = -1e30
LN_EPS = 1e-5
SWIGLU_ALPHA, LIMIT = 1.702, 7.0

CHUNKS = [
    [(0, 0, 0), (1, 0, 512)],
    [(2, 0, 0), (3, 0, 512)],
    [(0, 3, 0), (0, 1, 128), (1, 3, 512), (1, 1, 640)],
    [(2, 3, 0), (2, 1, 128), (3, 3, 512), (3, 1, 640)],
    [(0, 2, 0), (1, 2, 256), (2, 2, 512), (3, 2, 768)],
]
CHUNK_OF = {(h, kb): (c, col) for c, parts in enumerate(CHUNKS) for h, kb, col in parts}
MAX_BANKS = [[(h, 3, 0)] for h in range(4)] + [[(h, 2, 0), (h, 0, 384)] for h in range(4)] + [
    [(0, 1, 0), (1, 1, 256)], [(2, 1, 0), (3, 1, 256)]]
TRIANGLES = [(512, 2, 1), (512, 2, 1), (512, 2, 2), (512, 2, 2), (256, 4, 1)]


class Signal:

    def __init__(self, semaphore):
        self.semaphore, self.count = semaphore, 0


class Queue:

    def __init__(self):
        self.steps, self.waited = [], {}

    def add(self, make, waits=(), signal=None, by=1):
        fresh = []
        for point in waits:
            if point is None:
                continue
            sig, value = point
            if self.waited.get(id(sig), 0) < value:
                self.waited[id(sig)] = value
                fresh.append((sig.semaphore, value))
        self.steps.append((make, fresh, signal.semaphore if signal else None, by))
        if signal:
            signal.count += by
            return signal, signal.count
        return None

    def run(self, engine):
        for make, waits, semaphore, by in self.steps:
            for s, value in waits:
                engine.wait_ge(s, value)
            done = make(engine)
            if semaphore is not None:
                done.then_inc(semaphore, by)


def build_layer(nc, x, w_attn, b_attn, w_k2, b_k2, w_proj, b_proj,
                router_indices, routing_weights, w_up, b_up, w_down, b_down, out):
    batches, tokens, width = x.shape
    blocks = tokens // P
    halves = width // P
    heads_half = HEADS // halves
    experts, _, inter2 = w_up.shape
    inter = inter2 // 2
    routed = router_indices.shape[0]
    assert (tokens, width) == (512, 256) and routed == tokens and inter == width
    end_of_units = UNITS * batches

    ctx = ExitStack()
    with ctx:
        def sb(name, shape, dt=F32):
            return ctx.enter_context(nc.sbuf_tensor(name, shape, dt))

        def ps(name, cols):
            return ctx.enter_context(nc.psum_tensor(name, [P, cols], F32))

        def signal(name):
            return Signal(ctx.enter_context(nc.semaphore(name)))

        ident = sb("ident", [P, P])
        wq = sb("wq", [P, halves, 2 * halves, P])
        wk2 = sb("wk2", [P, halves, halves, P])
        wp = sb("wp", [P, halves, width])
        bias_qk = sb("bias_qk", [P, 3 * halves])
        bias2 = sb("bias2", [P, width])
        stack_q = [sb(f"stack_q{i}", [P, HEADS, tokens], BF16) for i in range(2)]
        stack_k = [sb(f"stack_k{i}", [P, HEADS, tokens], BF16) for i in range(2)]
        stack_k2 = [sb(f"stack_k2{i}", [P, HEADS, tokens], BF16) for i in range(2)]
        RING = 6
        prob = [sb(f"prob{i}", [P, 1024]) for i in range(RING)]
        value1 = sb("value1", [P, blocks, HEADS, 32])
        value2 = sb("value2", [P, blocks, HEADS, 32])
        x_in = [sb(f"x_in{i}", [P, blocks, width]) for i in range(2)]
        x_next = sb("x_next", [P, blocks, width])
        resid = sb("resid", [P, blocks, width])
        y_sum = [sb(f"y_sum{i}", [P, blocks, width]) for i in range(2)]
        y_second = [sb(f"y_second{i}", [P, blocks, GROUP, HEAD_DIM]) for i in range(2)]
        y_t = sb("y_t", [P, halves, tokens])
        x_t = sb("x_t", [P, halves, tokens])
        heads_t = sb("heads_t", [P, tokens])
        part_h = [sb(f"part_h{i}", [P, tokens], BF16) for i in range(2)]
        part_m = [sb(f"part_m{i}", [P, tokens], BF16) for i in range(2)]
        part_l = [sb(f"part_l{i}", [P, tokens], BF16) for i in range(2)]
        part_r = [sb(f"part_r{i}", [P, tokens]) for i in range(2)]
        max_cols = [sb(f"max_cols{i}", [P, 2, HEADS, blocks]) for i in range(2)]
        neg_h = sb("neg_h", [64, P], BF16)
        neg_m = sb("neg_m", [64, P], BF16)
        neg_l = sb("neg_l", [64, P], BF16)
        neg_r = sb("neg_r", [64, P])
        mask_rows = [sb(f"mask_rows{i}", [P, tokens], BF16) for i in range(2)]
        mask_first = sb("mask_first", [P, P], BF16)
        JUNK = 2
        junk = [sb(f"junk{i}", [P, tokens], BF16) for i in range(JUNK)]
        den = sb("den", [P, blocks, GROUP])
        rden = sb("rden", [P, blocks, GROUP])
        stats = sb("stats", [P, blocks, 6])
        mean_var = sb("mean_var", [P, blocks, 2])
        var_eps = sb("var_eps", [P, blocks])
        log_var = sb("log_var", [P, blocks])
        rstd = sb("rstd", [P, 5, blocks])
        shift = sb("shift", [P, blocks])
        eps_col = sb("eps_col", [P, 1])
        x1_routed = sb("x1_routed", [P, blocks, width])

        score_t = [ps(f"score_t{i}", 1024) for i in range(2)]
        score = [ps(f"score{i}", 512) for i in range(2)]
        out_t = ps("out_t", 512)
        misc = ps("misc", 512)

        s_loadw = signal("s_loadw")
        s_const = signal("s_const")
        s_consta = signal("s_consta")
        s_x = [signal(f"s_x{i}") for i in range(2)]
        s_next = signal("s_next")
        s_resid_in = signal("s_resid_in")
        s_stack = {(kind, hf): signal(f"s_stack_{kind}{hf}") for kind in ("q", "k", "k2") for hf in range(halves)}
        s_maxrow = [signal(f"s_maxrow{i}") for i in range(2)]
        s_out = signal("s_out")
        s_score_t = signal("s_score_t")
        s_score = signal("s_score")
        s_pv = signal("s_pv")
        s_pe = signal("s_pe")
        s_exp = signal("s_exp")
        s_act = signal("s_act")
        s_max = signal("s_max")
        s_dve = signal("s_dve")
        s_mask = signal("s_mask")
        s_pool = signal("s_pool")
        s_ffn_w = [signal(f"s_ffn_w{i}") for i in range(2)]
        s_ffn_in = signal("s_ffn_in")

        pe, act, dve, pool, sp = (Queue() for _ in range(5))

        raw_attn = prob[0][:, :].rearrange("p (h n) -> p h n", h=halves)
        raw_k2 = prob[1][:, 0:halves * width].rearrange("p (h n) -> p h n", h=halves)
        raw_bias = prob[2][:, 0:width]
        sp.add(lambda e: e.dma_start(raw_attn, w_attn.rearrange("(h p) n -> p h n", p=P)), signal=s_loadw, by=16)
        sp.add(lambda e: e.dma_start(raw_k2, w_k2.rearrange("(h p) n -> p h n", p=P)), signal=s_loadw, by=16)
        sp.add(lambda e: e.dma_start(wp[:, :, :], w_proj.rearrange("(h p) n -> p h n", p=P)), signal=s_loadw, by=16)
        sp.add(lambda e: e.dma_start(raw_bias, b_proj.rearrange("(o n) -> o n", o=1).to_broadcast([P, width])),
               signal=s_loadw, by=16)
        bias_rows = prob[3][0:3 * halves, 0:P]
        bias_sorted = prob[3][0:3 * halves, P:2 * P]
        sp.add(lambda e: e.dma_start(prob[3][0:2 * halves, 0:P], b_attn.rearrange("(r p) -> r p", p=P)), signal=s_loadw, by=16)
        sp.add(lambda e: e.dma_start(prob[3][2 * halves:3 * halves, 0:P], b_k2.rearrange("(r p) -> r p", p=P)), signal=s_loadw, by=16)
        weights_loaded = (s_loadw, s_loadw.count)

        pool.add(lambda e: e.memset(ident[:, :], 1.0), signal=s_const)
        made = pool.add(lambda e: e.memset(x_next[:, :, :], 0.0), signal=s_const)
        next_zeroed = made
        pool.add(lambda e: e.memset(value1[:, :, :, :], 1.0), signal=s_const)
        pool.add(lambda e: e.memset(value2[:, :, :, :], 1.0), signal=s_const)
        for tile in (mask_rows[0], mask_rows[1], mask_first):
            pool.add(lambda e, tile=tile: e.memset(tile[:, :], 0.0), signal=s_const)
        made = pool.add(lambda e: e.memset(eps_col[:, :], LN_EPS), signal=s_const)
        pool.add(lambda e: e.affine_select(out=ident[:, :], in_=ident[:, :], compare_op=ALU.is_equal, fill=0.0,
                                           base=0, pattern=[[1, P]], channel_multiplier=-1),
                 waits=[made], signal=s_const)
        for a in range(2):
            tri = mask_rows[a][:, tokens - P:tokens]
            pool.add(lambda e, tri=tri, a=a: e.affine_select(
                out=tri, in_=tri, compare_op=ALU.is_ge, fill=MASKED, base=-a, pattern=[[-1, P]],
                channel_multiplier=1), signal=s_const)
        made = pool.add(lambda e: e.affine_select(
            out=mask_first[:, :], in_=mask_first[:, :], compare_op=ALU.is_ge, fill=MASKED, base=-1,
            pattern=[[-1, P]], channel_multiplier=1), signal=s_const)
        constants = made

        R = SCORE_ROWS
        for i in range(2):
            dve.add(lambda e, i=i: e.memset(stack_k2[i][R:R + 2 * MAX_PARTS, :, :], 1.0), signal=s_consta)
            rows_made = dve.add(lambda e, i=i: e.memset(stack_k[i][R:R + MAX_PARTS, :, :], 1.0), signal=s_consta)
        for i in range(2):
            rows_made = dve.add(lambda e, i=i: e.memset(stack_k2[i][R:R + MAX_PARTS, :, :], 0.0),
                            waits=[rows_made], signal=s_consta)
        dve.add(lambda e: e.memset(mask_first[0:1, 0:1], 0.0), waits=[constants], signal=s_consta)
        for piece in range(2 * halves):
            made = dve.add(lambda e, piece=piece: e.tensor_copy(
                wq[:, :, piece, :].rearrange("p c (d h) -> p c d h", d=HEAD_DIM),
                raw_attn[:, :, piece * P:(piece + 1) * P].rearrange("p c (h d) -> p c d h", d=HEAD_DIM)),
                waits=[weights_loaded], signal=s_consta)
        for hf in range(halves):
            made = dve.add(lambda e, hf=hf: e.tensor_copy(
                wk2[:, :, hf, :].rearrange("p c (d h) -> p c d h", d=HEAD_DIM),
                raw_k2[:, :, hf * P:(hf + 1) * P].rearrange("p c (h d) -> p c d h", d=HEAD_DIM)),
                signal=s_consta)
        dve.add(lambda e: e.tensor_tensor(bias2[:, :], raw_bias, raw_bias, ALU.add), signal=s_consta)
        made = dve.add(lambda e: e.tensor_copy(bias_sorted.rearrange("r (d h) -> r d h", d=HEAD_DIM),
                                               bias_rows.rearrange("r (h d) -> r d h", d=HEAD_DIM)), signal=s_consta)
        made = pe.add(lambda e: e.transpose(misc[:, 0:3 * halves], bias_sorted, ident[0:3 * halves, 0:3 * halves]),
                      waits=[made, constants], signal=s_pe)
        weights_ready = dve.add(lambda e: e.tensor_copy(bias_qk[:, :], misc[:, 0:3 * halves]), waits=[made], signal=s_consta)

        x_loaded, next_loaded, resid_loaded = {}, {}, {}
        x_t_ready = {}
        x_t_read = {}
        stack_ready = {}
        unit_scores_done = {}
        unit_max_done = {}
        unit_max_scores = {}
        max_rows_ready = {}
        exp_done, mask_done = {}, {}
        chunk_read = {}
        bank_max = {}
        unit_pv_done = {}
        heads_copied = {}
        value1_ready, value2_ready = {}, {}
        y_added = {}
        state = {"misc_read": [weights_ready, constants], "junk": [None] * JUNK, "piece": 0, "heads_read": None,
                 "max_copied": None, "neg_sent": None, "den": None, "y_t_read": None,
                 "resid_free": None, "value1_free": None, "x_free": {}, "next_free": next_zeroed,
                 "neg_r": None}
        piece_history = []

        def unit_parts(unit):
            return unit // UNITS, unit % UNITS // GROUPS, unit % GROUPS

        def load_x(b):
            x_loaded[b] = sp.add(lambda e: e.dma_start(x_in[b % 2][:, :, :], x[b].rearrange("(t p) c -> p t c", p=P)),
                                 waits=[state["x_free"].get(b)], signal=s_x[b % 2], by=16)

        def load_next(b):
            last = blocks - 1
            sp.add(lambda e: e.dma_start(x_next[:, 0:last, :], x[b, 1:1 + last * P, :].rearrange("(t p) c -> p t c", p=P)),
                   waits=[state["next_free"]], signal=s_next, by=16)
            next_loaded[b] = sp.add(lambda e: e.dma_start(x_next[0:P - 1, last, :], x[b, 1 + last * P:tokens, :]),
                                    signal=s_next, by=16)

        def load_resid(b):
            resid_loaded[b] = sp.add(lambda e: e.dma_start(resid[:, :, :], x[b].rearrange("(t p) c -> p t c", p=P)),
                                     waits=[state["resid_free"]], signal=s_resid_in, by=16)

        def transpose_x(b, hf):
            src = x_in[b % 2]
            for t in range(blocks):
                done = pe.add(lambda e, t=t: e.transpose(misc[:, t * P:(t + 1) * P], src[:, t, hf * P:(hf + 1) * P], ident[:, :]),
                              waits=[x_loaded[b]] + state["misc_read"], signal=s_pe if t == blocks - 1 else None)
            copied = act.add(lambda e: e.activation(x_t[:, hf, :], misc[:, :], ACT.Copy),
                             waits=[done, x_t_read.get(b - 1)], signal=s_act)
            state["misc_read"] = [copied]
            x_t_ready[b] = copied

        def project_piece(kind, b, hf):
            n = state["piece"]
            state["piece"] += 1
            i = n % 2
            old = piece_history[n - 2] if n >= 2 else {}
            piece = {"q": hf, "k": halves + hf, "k2": 2 * halves + hf}[kind]
            for c in range(halves):
                w = wk2[:, c, hf, :] if kind == "k2" else wq[:, c, piece, :]
                done = pe.add(lambda e, c=c, w=w: e.matmul(misc[:, :], w, x_t[:, c, :], start=(c == 0), stop=(c == halves - 1)),
                              waits=[x_t_ready[b], weights_ready] + state["misc_read"],
                              signal=s_pe if c == halves - 1 else None)
            x_t_read[b] = done
            bias = bias_qk[:, piece:piece + 1]
            high = act.add(lambda e: e.activation(part_h[i][:, :], misc[:, :], ACT.Identity, bias=bias),
                           waits=[done, weights_ready, old.get("sent")], signal=s_act)
            rest = dve.add(lambda e: e.scalar_tensor_tensor(out=part_r[i][:, :], in0=misc[:, :], scalar=bias,
                                                            in1=part_h[i][:, :], op0=ALU.add, op1=ALU.subtract),
                           waits=[high, old.get("low")], signal=s_dve)
            state["misc_read"] = [rest]
            middle = pool.add(lambda e: e.tensor_copy(part_m[i][:, :], part_r[i][:, :]),
                              waits=[rest, old.get("sent")], signal=s_pool)
            low = pool.add(lambda e: e.tensor_tensor(part_l[i][:, :], part_r[i][:, :], part_m[i][:, :], ALU.subtract),
                           waits=[middle, old.get("sent")], signal=s_pool)
            stack = {"q": stack_q, "k": stack_k, "k2": stack_k2}[kind][b % 2]
            parts = (part_h[i], part_m[i], part_l[i])
            last_group = (hf + 1) * GROUPS // halves - 1
            reader = UNITS * (b - 2) + (0 if kind == "k" else GROUPS) + last_group
            free = unit_scores_done.get(reader)
            for term, part in enumerate(PARTS_Q if kind == "q" else PARTS_K):
                sent = sp.add(lambda e, term=term, part=part: e.dma_start(
                    stack[term * HEAD_DIM:(term + 1) * HEAD_DIM, hf * heads_half:(hf + 1) * heads_half, :],
                    parts[part][:, :]), waits=[low, free, constants], signal=s_stack[kind, hf], by=16)
            stack_ready[kind, b, hf] = sent
            piece_history.append({"sent": sent, "low": low})

        def stacks(unit):
            b, a, g = unit_parts(unit)
            kind = "k2" if a else "k"
            keys = (stack_k2 if a else stack_k)[b % 2]
            hf = g * halves // GROUPS
            return stack_q[b % 2], keys, [stack_ready["q", b, hf], stack_ready[kind, b, hf]]

        def max_bank(unit, n):
            b, a, g = unit_parts(unit)
            queries, keys, ready = stacks(unit)
            number = len(MAX_BANKS) * unit + n
            bank = score[number % 2]
            for h, qb, col in MAX_BANKS[n]:
                head, keys_n = GROUP * g + h, P * (qb + 1)
                last = (h, qb, col) == MAX_BANKS[n][-1]
                done = pe.add(lambda e, head=head, qb=qb, col=col, keys_n=keys_n: e.matmul(
                    bank[:, col:col + keys_n], queries[0:SCORE_ROWS, head, qb * P:(qb + 1) * P],
                    keys[0:SCORE_ROWS, head, 0:keys_n], start=True, stop=True),
                    waits=ready + [bank_max.get(number - 2)], signal=s_score if last else None)
            unit_max_scores[unit] = done
            for h, qb, col in MAX_BANKS[n]:
                head, keys_n = GROUP * g + h, P * (qb + 1)
                mask = mask_first[:, :] if a and qb == 0 else mask_rows[a][:, tokens - keys_n:tokens]
                k = s_max.count % JUNK
                target = max_cols[b % 2]
                state["junk"][k] = bank_max[number] = dve.add(
                    lambda e, head=head, qb=qb, col=col, keys_n=keys_n, mask=mask, k=k: e.tensor_tensor_reduce(
                        junk[k][:, 0:keys_n], bank[:, col:col + keys_n], mask, 1.0, -3e38, ALU.add, ALU.max,
                        target[:, a, head, qb:qb + 1]),
                    waits=[done, constants, state["junk"][k]], signal=s_max)
            unit_max_done[unit] = bank_max[number]

        def negate_maxima(b, a):
            src = max_cols[b % 2][:, a, :, :].rearrange("p h q -> p (h q)")
            n = HEADS * blocks
            done = pe.add(lambda e: e.transpose(misc[0:n, 0:P], src, ident[:, :]),
                          waits=[unit_max_done[UNITS * b + GROUPS * a + GROUPS - 1]] + state["misc_read"], signal=s_pe)
            high = act.add(lambda e: e.activation(neg_h[:, :], misc[0:n, 0:P], ACT.Copy, scale=-1.0),
                           waits=[done, state["neg_sent"]], signal=s_act)
            rest = dve.add(lambda e: e.scalar_tensor_tensor(out=neg_r[:, :], in0=misc[0:n, 0:P], scalar=-1.0,
                                                            in1=neg_h[:, :], op0=ALU.mult, op1=ALU.subtract),
                           waits=[high, state["neg_r"]], signal=s_dve)
            state["misc_read"] = [rest]
            middle = pool.add(lambda e: e.tensor_copy(neg_m[:, :], neg_r[:, :]),
                              waits=[rest, state["neg_sent"]], signal=s_pool)
            low = pool.add(lambda e: e.tensor_tensor(neg_l[:, :], neg_r[:, :], neg_m[:, :], ALU.subtract),
                           waits=[middle], signal=s_pool)
            state["neg_r"] = low
            free = unit_scores_done.get(UNITS * (b - 2) + UNITS - 1)
            for part, tile in enumerate((neg_h, neg_m, neg_l)):
                row = SCORE_ROWS + MAX_PARTS * a + part
                sent = sp.add(lambda e, row=row, tile=tile: e.dma_start(stack_q[b % 2][row:row + 1, :, :], tile[:, :]),
                              waits=[low, free], signal=s_maxrow[a], by=16)
            max_rows_ready[b, a] = state["neg_sent"] = sent

        def chunk(unit, c):
            b, a, g = unit_parts(unit)
            queries, keys, ready = stacks(unit)
            number = SLOTS * unit + c
            bank = score_t[number % 2]
            rows = SCORE_ROWS + MAX_PARTS * (a + 1)
            ready = ready + [max_rows_ready[b, 0], max_rows_ready[b, a]]
            for h, kb, col in CHUNKS[c]:
                head, queries_n = GROUP * g + h, tokens - P * kb
                last = (h, kb, col) == CHUNKS[c][-1]
                done = pe.add(lambda e, head=head, kb=kb, col=col, queries_n=queries_n: e.matmul(
                    bank[:, col:col + queries_n], keys[0:rows, head, kb * P:(kb + 1) * P],
                    queries[0:rows, head, kb * P:tokens], start=True, stop=True),
                    waits=ready + [exp_done.get(number - 2)], signal=s_score_t if last else None)
            unit_scores_done[unit] = done
            tile = prob[number % RING]
            exp_done[number] = act.add(
                lambda e: e.activation(tile[:, :], bank[:, :], ACT.Exp, scale=1.0 / np.sqrt(HEAD_DIM).item()),
                waits=[done, chunk_read.get(number - RING), weights_ready], signal=s_exp)
            step, runs, cut = TRIANGLES[c]
            view = tile[:, :].rearrange("p (r s) -> p r s", s=step)[:, :, 0:cut * P]
            pattern = [[0, runs], [0, cut], [1, P]]
            mask_done[number] = pool.add(lambda e: e.affine_select(
                out=view, in_=view, compare_op=ALU.is_ge, fill=0.0, base=-a, pattern=pattern,
                channel_multiplier=-1), waits=[exp_done[number]], signal=s_mask)

        def weigh(unit, kb, first, count, start=False, stop=False):
            b, a, g = unit_parts(unit)
            value = value2 if a else value1
            ready = value2_ready[b, g] if a else value1_ready[b]
            for h in range(GROUP):
                c, col = CHUNK_OF[h, kb]
                number = SLOTS * unit + c
                at = col + first - P * kb
                done = pe.add(lambda e, h=h, number=number, at=at: e.matmul(
                    out_t[32 * h:32 * h + 32, first:first + count], value[:, kb, GROUP * g + h, :],
                    prob[number % RING][:, at:at + count], start=start, stop=stop, skip_group_check=True),
                    waits=[mask_done[number], ready, heads_copied.get(unit - 1)],
                    signal=s_pv if h == GROUP - 1 else None)
            return done

        def weigh_slot(slot, unit):
            if slot == 4 and 0 <= unit < end_of_units:
                weigh(unit, 0, 0, 256, start=True)
            before = unit - 1
            if not 0 <= before < end_of_units:
                return
            number = SLOTS * before
            if slot == 0:
                chunk_read[number] = chunk_read[number + 1] = weigh(before, 0, 256, 256)
            if slot == 1:
                weigh(before, 1, P, 3 * P)
            if slot == 2:
                chunk_read[number + 2] = chunk_read[number + 3] = weigh(before, 3, 3 * P, P)
                chunk_read[number + 4] = unit_pv_done[before] = weigh(before, 2, 2 * P, 2 * P, stop=True)

        def finish_unit(unit):
            b, a, g = unit_parts(unit)
            heads_copied[unit] = act.add(lambda e: e.activation(heads_t[:, :], out_t[:, :], ACT.Copy),
                                         waits=[unit_pv_done[unit], state["heads_read"]], signal=s_act)
            for t in range(blocks):
                done = pe.add(lambda e, t=t: e.transpose(misc[:, t * P:(t + 1) * P], heads_t[:, t * P:(t + 1) * P], ident[:, :]),
                              waits=[heads_copied[unit]] + state["misc_read"], signal=s_pe if t == blocks - 1 else None)
            state["heads_read"] = done
            heads = misc[:, :].rearrange("p (t h w) -> p t h w", t=blocks, h=GROUP)
            floor = dve.add(lambda e: e.tensor_scalar(den[:, :, :], heads[:, :, :, HEAD_DIM], 1e-30, None, ALU.max),
                            waits=[done, state["den"]], signal=s_dve)
            inverse = dve.add(lambda e: e.reciprocal(rden[:, :, :], den[:, :, :]), waits=[floor], signal=s_dve)
            wide = bass.AP(rden[:, :, :].tensor, rden[:, :, :].offset,
                           [list(rden[:, :, :].ap[0]), [GROUP, blocks], [1, GROUP], [0, HEAD_DIM]])
            chans = slice(g * GROUP * HEAD_DIM, (g + 1) * GROUP * HEAD_DIM)
            y = y_sum[b % 2][:, :, chans].rearrange("p t (h d) -> p t h d", d=HEAD_DIM)
            if a == 0:
                normal = dve.add(lambda e: e.tensor_tensor(y, heads[:, :, :, 0:HEAD_DIM], wide, ALU.mult),
                                 waits=[inverse, state.get(("y_t", b - 2))], signal=s_dve)
                nxt = x_next[:, :, chans].rearrange("p t (h d) -> p t h d", d=HEAD_DIM)
                value2_ready[b, g] = pool.add(lambda e: e.tensor_tensor(
                    value2[:, :, GROUP * g:GROUP * g + GROUP, 0:HEAD_DIM], nxt, y, ALU.subtract),
                    waits=[normal, next_loaded[b], constants, unit_pv_done.get(UNITS * (b - 1) + GROUPS + g)], signal=s_pool)
                state["next_free"] = value2_ready[b, g]
            else:
                second = y_second[g % 2]
                normal = dve.add(lambda e: e.tensor_tensor(second[:, :, :, :], heads[:, :, :, 0:HEAD_DIM], wide, ALU.mult),
                                 waits=[inverse, state.get(("second", g % 2))], signal=s_dve)
                y_added[b] = pool.add(lambda e: e.tensor_tensor(y, y, second[:, :, :, :], ALU.add),
                                      waits=[normal, value2_ready[b, g]], signal=s_pool)
                state["second", g % 2] = y_added[b]
            state["den"] = normal
            state["misc_read"] = [normal]

        def transpose_y(b, hf):
            src = y_sum[b % 2]
            for t in range(blocks):
                done = pe.add(lambda e, t=t: e.transpose(misc[:, t * P:(t + 1) * P], src[:, t, hf * P:(hf + 1) * P], ident[:, :]),
                              waits=[y_added[b]] + state["misc_read"], signal=s_pe if t == blocks - 1 else None)
            state["y_t", b] = done
            state["y_t_ready"] = act.add(lambda e: e.activation(y_t[:, hf, :], misc[:, :], ACT.Copy),
                                         waits=[done, state["y_t_read"]], signal=s_act)
            state["misc_read"] = [state["y_t_ready"]]

        def project_out(b, pair):
            for j in range(2):
                t = 2 * pair + j
                for c in range(halves):
                    done = pe.add(lambda e, t=t, j=j, c=c: e.matmul(
                        misc[:, j * width:(j + 1) * width], y_t[:, c, t * P:(t + 1) * P], wp[:, c, :],
                        start=(c == 0), stop=(c == halves - 1)),
                        waits=[state["y_t_ready"], weights_loaded] + state["misc_read"],
                        signal=s_pe if (j, c) == (1, halves - 1) else None)
            state["y_t_read"] = done
            rows = resid[:, 2 * pair:2 * pair + 2, :]
            state["attended"] = dve.add(lambda e: e.tensor_tensor(
                rows, misc[:, :].rearrange("p (t c) -> p t c", t=2), rows, ALU.add),
                waits=[done, state["biased"]], signal=s_dve)
            state["misc_read"] = [state["attended"]]

        def add_bias(b):
            wide = bass.AP(bias2[:, :].tensor, bias2[:, :].offset, [list(bias2[:, :].ap[0]), [0, blocks], [1, width]])
            state["biased"] = pool.add(lambda e: e.tensor_tensor(resid[:, :, :], resid[:, :, :], wide, ALU.add),
                                       waits=[resid_loaded[b], weights_ready], signal=s_pool)

        def norm_stats(tile, ready):
            for t in range(blocks):
                done = dve.add(lambda e, t=t: e.bn_stats(stats[:, t, :], tile[:, t, :]),
                               waits=[ready, state.get("aggregated")], signal=s_dve)
            for t in range(blocks):
                done = dve.add(lambda e, t=t: e.bn_aggr(mean_var[:, t, :], stats[:, t, :]),
                               waits=[done, state.get("shifted")], signal=s_dve)
            state["aggregated"] = done
            return done

        def norm_rstd(aggregated):
            var = mean_var[:, :, 1]
            v = pool.add(lambda e: e.tensor_scalar(var_eps[:, :], var, LN_EPS, None, ALU.add),
                         waits=[aggregated], signal=s_pool)
            log = act.add(lambda e: e.activation(log_var[:, :], var_eps[:, :], ACT.Ln), waits=[v], signal=s_act)
            guess = act.add(lambda e: e.activation(rstd[:, 0, :], log_var[:, :], ACT.Exp, scale=-0.5),
                            waits=[log, state.get("shifted")], signal=s_act)
            s = pool.add(lambda e: e.tensor_tensor(rstd[:, 1, :], rstd[:, 0, :], rstd[:, 0, :], ALU.mult),
                         waits=[guess], signal=s_pool)
            s = pool.add(lambda e: e.tensor_tensor(rstd[:, 2, :], rstd[:, 1, :], var_eps[:, :], ALU.mult),
                         waits=[s], signal=s_pool)
            s = pool.add(lambda e: e.tensor_scalar(rstd[:, 3, :], rstd[:, 2, :], -0.5, 1.5, ALU.mult, ALU.add),
                         waits=[s], signal=s_pool)
            s = pool.add(lambda e: e.tensor_tensor(rstd[:, 4, :], rstd[:, 3, :], rstd[:, 0, :], ALU.mult),
                         waits=[s, state.get("applied")], signal=s_pool)
            s = pool.add(lambda e: e.tensor_tensor(log_var[:, :], mean_var[:, :, 0], rstd[:, 4, :], ALU.mult),
                         waits=[s], signal=s_pool)
            s = pool.add(lambda e: e.tensor_scalar(shift[:, :], log_var[:, :], -1.0, None, ALU.mult),
                         waits=[s], signal=s_pool)
            state["shifted"] = s
            return s

        def norm_apply(dst, src, ready):
            for t in range(blocks):
                done = act.add(lambda e, t=t: e.activation(dst[:, t, :], src[:, t, :], ACT.Identity,
                                                           bias=shift[:, t:t + 1], scale=rstd[:, 4, t:t + 1]),
                               waits=[ready], signal=s_act)
            state["applied"] = done
            return done

        def store(b, ready):
            state["resid_free"] = sp.add(lambda e: e.dma_start(out[b].rearrange("(t p) c -> p t c", p=P), resid[:, :, :]),
                                         waits=[ready], signal=s_out, by=16)

        def extra(unit, slot):
            place = unit % UNITS
            ahead = (unit - place) // UNITS
            pieces = {5: ("k", 0), 6: ("q", 0), 7: ("k", 1), 0: ("q", 1), 1: ("k2", 0), 2: ("k2", 1)}
            if slot == 0 and place in pieces:
                b = ahead + (2 if place >= 5 else 1)
                if 0 <= b < batches:
                    project_piece(pieces[place][0], b, pieces[place][1])
            if slot == 0 and place in (3, 4) and 0 <= ahead + 2 < batches:
                transpose_x(ahead + 2, place - 3)
            if slot == 2 and place == 6 and 0 <= ahead + 1 < batches:
                negate_maxima(ahead + 1, 0)
            if slot == 2 and place == 2 and 0 <= ahead < batches:
                negate_maxima(ahead, 1)
            if place == 5 and slot == 3 and 0 <= ahead + 1 < batches:
                b = ahead + 1
                value1_ready[b] = pool.add(lambda e: e.tensor_copy(
                    value1[:, :, :, 0:HEAD_DIM], x_in[b % 2][:, :, :].rearrange("p t (h d) -> p t h d", d=HEAD_DIM)),
                    waits=[x_loaded[b], constants, unit_pv_done.get(UNITS * (b - 1) + GROUPS - 1)], signal=s_pool)
                state["x_free"][b + 2] = value1_ready[b]
                load_next(b)
                if b + 2 < batches:
                    load_x(b + 2)
            b = ahead - 1
            if not 0 <= b < batches:
                return
            if (place, slot) == (0, 0):
                load_resid(b)
            if (place, slot) == (1, 0):
                add_bias(b)
            if slot == 2 and place in (1, 3):
                transpose_y(b, place // 2)
            if slot == 2 and place in (4, 5):
                project_out(b, place - 4)
            if (place, slot) == (6, 0):
                state["ln"] = norm_rstd(norm_stats(resid, state["attended"]))
            if (place, slot) == (6, 2):
                state["x1"] = norm_apply(x1_routed if b == 0 else resid, resid, state["ln"])
                if b == 0:
                    state["resid_free"] = state["x1_routed"] = state["x1"]
            if b == 0:
                return
            if (place, slot) == (7, 0):
                state["ln"] = norm_rstd(norm_stats(resid, state["x1"]))
            if (place, slot) == (7, 2):
                store(b, norm_apply(resid, resid, state["ln"]))

        act.add(lambda e: e.preload_act_table_set("natural_log_exp_and_others") or None)
        load_x(0)
        if batches > 1:
            load_x(1)
        for unit in range(-2 * UNITS + 3, end_of_units + UNITS):
            for slot in range(SLOTS):
                if 0 <= unit < end_of_units:
                    chunk(unit, slot)
                if 0 <= unit + LEAD < end_of_units:
                    max_bank(unit + LEAD, 2 * slot)
                    max_bank(unit + LEAD, 2 * slot + 1)
                weigh_slot(slot, unit)
                extra(unit, slot)
                if slot == 3 and 0 <= unit - 1 < end_of_units:
                    finish_unit(unit - 1)

        free = unit_scores_done[end_of_units - 1]

        def in_stack(stack, first, shape):
            n = int(np.prod(shape))
            flat = stack[:, :, :].rearrange("p h t -> p (h t)")[:, 2 * first:2 * (first + n)].bitcast(F32)
            names = "abcd"[:len(shape)]
            sizes = dict(zip(names, shape))
            return flat.rearrange(f"p ({' '.join(names)}) -> p {' '.join(names)}", **sizes)

        up_w = [in_stack(stack_k[i], 0, (halves, inter2)) for i in range(2)]
        down_w = [in_stack(stack_k[i], halves * inter2, (halves, width)) for i in range(2)]
        x1_t = in_stack(stack_q[0], 0, (halves, tokens))
        gate = [in_stack(stack_q[0], (2 + i) * 512, (tokens,)) for i in range(2)]
        sigm = [in_stack(stack_q[0], (4 + i) * 512, (tokens,)) for i in range(2)]
        lift = [in_stack(stack_q[0], (6 + i) * 512, (tokens,)) for i in range(2)]
        inner = [in_stack(stack_q[1], 1024 * i, (halves, tokens)) for i in range(2)]
        ffn = in_stack(stack_q[1], 2048, (blocks, width))
        down_b = in_stack(stack_k2[0], 0, (width,))
        up_b = in_stack(stack_k2[0], 256, (experts * inter2 // P,))
        chosen = in_stack(stack_k2[0], 512, (blocks, 2))
        same = in_stack(stack_k2[0], 528, (blocks, 2))
        route = in_stack(stack_k2[0], 544, (blocks, experts))
        coef = in_stack(stack_k2[0], 576, (blocks, experts))
        coef_t = in_stack(stack_k2[0], 1024, (tokens,))
        up_b_rows = in_stack(stack_k2[0], 1536, (P,))
        chosen_i = chosen_raw = in_stack(stack_k2[0], 1664, (blocks, 2)).bitcast(I32)

        def load_expert(ex, waits):
            i = ex % 2
            sp.add(lambda e: e.dma_start(up_w[i], w_up[ex].rearrange("(h p) n -> p h n", p=P)),
                   waits=waits, signal=s_ffn_w[i], by=16)
            return sp.add(lambda e: e.dma_start(down_w[i], w_down[ex].rearrange("(h p) n -> p h n", p=P)),
                          signal=s_ffn_w[i], by=16)

        n_rows = experts * inter2 // P
        sp.add(lambda e: e.dma_start(chosen_i, router_indices.rearrange("(t p) k -> p t k", p=P)),
               waits=[free], signal=s_ffn_in, by=16)
        sp.add(lambda e: e.dma_start(route, routing_weights.rearrange("(t p) k -> p t k", p=P)), signal=s_ffn_in, by=16)
        sp.add(lambda e: e.dma_start(down_b[0:experts, :], b_down), signal=s_ffn_in, by=16)
        ffn_loaded = sp.add(lambda e: e.dma_start(up_b_rows[0:n_rows, :], b_up.rearrange("x (r p) -> (x r) p", p=P)),
                            signal=s_ffn_in, by=16)
        expert_loaded = {ex: load_expert(ex, []) for ex in range(2)}

        step = dve.add(lambda e: e.tensor_copy(chosen, chosen_i), waits=[ffn_loaded, free], signal=s_dve)
        for ex in range(experts):
            step = dve.add(lambda e, ex=ex: e.tensor_scalar(same, chosen, float(ex), None, ALU.is_equal),
                           waits=[step], signal=s_dve)
            step = dve.add(lambda e, ex=ex: e.tensor_tensor(coef[:, :, ex], same[:, :, 0], same[:, :, 1], ALU.add),
                           waits=[step], signal=s_dve)
        coef_ready = dve.add(lambda e: e.tensor_tensor(coef, coef, route, ALU.mult), waits=[step], signal=s_dve)

        for hf in range(halves):
            for t in range(blocks):
                done = pe.add(lambda e, t=t, hf=hf: e.transpose(misc[:, t * P:(t + 1) * P], x1_routed[:, t, hf * P:(hf + 1) * P], ident[:, :]),
                              waits=[state["x1_routed"]] + state["misc_read"], signal=s_pe if t == blocks - 1 else None)
            x1_t_ready = act.add(lambda e, hf=hf: e.activation(x1_t[:, hf, :], misc[:, :], ACT.Copy), waits=[done, free], signal=s_act)
            state["misc_read"] = [x1_t_ready]
        gates_rows = up_b_rows[0:n_rows, :].rearrange("r (c two) -> r two c", two=2)
        for two in range(2):
            done = pe.add(lambda e, two=two: e.transpose(misc[0:64, two * n_rows:(two + 1) * n_rows], gates_rows[:, two, :], ident[0:n_rows, 0:n_rows]),
                          waits=[ffn_loaded] + state["misc_read"], signal=s_pe if two else None)
        bias_lo = act.add(lambda e: e.activation(up_b[0:64, :].rearrange("p (w x f) -> p w x f", w=2, x=experts),
                                                 misc[0:64, 0:2 * n_rows].rearrange("p (w x f two) -> p w x f two", w=2, x=experts, two=2)[:, :, :, :, 0],
                                                 ACT.Copy), waits=[done, free], signal=s_act)
        state["misc_read"] = [bias_lo]
        odd = in_stack(stack_k2[0], 1792, (n_rows,))
        odd_copy = act.add(lambda e: e.activation(odd[0:64, :].rearrange("p (w x f) -> p w x f", w=2, x=experts),
                                                  misc[0:64, 0:2 * n_rows].rearrange("p (w x f two) -> p w x f two", w=2, x=experts, two=2)[:, :, :, :, 1],
                                                  ACT.Copy), waits=[done], signal=s_act)
        state["misc_read"] = [odd_copy]
        up_b_ready = sp.add(lambda e: e.dma_start(up_b[64:128, :], odd[0:64, :]), waits=[odd_copy, bias_lo], signal=s_ffn_in, by=16)
        for t in range(blocks):
            done = pe.add(lambda e, t=t: e.transpose(misc[0:experts, t * P:(t + 1) * P], coef[:, t, :], ident[:, :]),
                          waits=[coef_ready] + state["misc_read"], signal=s_pe if t == blocks - 1 else None)
        coef_t_ready = act.add(lambda e: e.activation(coef_t[0:experts, :], misc[0:experts, :], ACT.Copy),
                               waits=[done, free], signal=s_act)
        state["misc_read"] = [coef_t_ready]
        ffn_done = None
        for pair in range(2):
            for j in range(2):
                t = 2 * pair + j
                done = pe.add(lambda e, t=t, j=j: e.matmul(misc[:, j * width:(j + 1) * width], coef_t[0:experts, t * P:(t + 1) * P],
                                                           down_b[0:experts, :], start=True, stop=True),
                              waits=[coef_t_ready] + state["misc_read"], signal=s_pe if j else None)
            rows = slice(2 * pair, 2 * pair + 2)
            ffn_done = dve.add(lambda e, rows=rows: e.tensor_tensor(
                ffn[:, rows, :], misc[:, :].rearrange("p (t c) -> p t c", t=2), x1_routed[:, rows, :], ALU.add),
                waits=[done, state["x1_routed"], free], signal=s_dve)
            state["misc_read"] = [ffn_done]

        gate_banks = [score_t[i][:, 0:512] for i in range(2)]
        up_banks = [score_t[i][:, 512:1024] for i in range(2)]
        down_banks = [score[0], score[1]]
        last_exp = exp_done[SLOTS * end_of_units - 1]
        last_max = unit_max_done[end_of_units - 1]
        bank_read, buffers, inner_read, down_read = {}, {}, {}, {}
        for ex in range(experts):
            w = up_w[ex % 2]
            for f in range(halves):
                n = halves * ex + f
                i = n % 2
                for two, bank in enumerate((gate_banks[i], up_banks[i])):
                    for c in range(halves):
                        done = pe.add(lambda e, w=w, c=c, f=f, two=two, bank=bank: e.matmul(
                            bank, w[:, c, 2 * P * f + two:2 * P * (f + 1):2], x1_t[:, c, :],
                            start=(c == 0), stop=(c == halves - 1)),
                            waits=[expert_loaded[ex], x1_t_ready, last_exp, bank_read.get(n - 2)],
                            signal=s_pe if (two, c) == (1, halves - 1) else None)
                bg = up_b[:, ex * halves + f:ex * halves + f + 1]
                bu = up_b[:, (experts + ex) * halves + f:(experts + ex) * halves + f + 1]
                old = buffers.get(n - 2)
                gated = dve.add(lambda e, i=i, bg=bg: e.tensor_scalar(gate[i], gate_banks[i], bg, LIMIT, ALU.add, ALU.min),
                                waits=[done, up_b_ready, old], signal=s_dve)
                lifted = dve.add(lambda e, i=i, bu=bu: e.tensor_scalar(lift[i], up_banks[i], bu, LIMIT, ALU.add, ALU.min),
                                 waits=[old], signal=s_dve)
                bank_read[n] = lifted
                sig = act.add(lambda e, i=i: e.activation(sigm[i], gate[i], ACT.Sigmoid, scale=SWIGLU_ALPHA),
                              waits=[gated, old], signal=s_act)
                lifted = dve.add(lambda e, i=i: e.tensor_scalar(lift[i], lift[i], -LIMIT, 1.0, ALU.max, ALU.add),
                                 waits=[lifted], signal=s_dve)
                glu = pool.add(lambda e, i=i: e.tensor_tensor(sigm[i], gate[i], sigm[i], ALU.mult), waits=[sig, gated], signal=s_pool)
                buffers[n] = dve.add(lambda e, i=i, ex=ex, f=f: e.tensor_tensor(inner[ex % 2][:, f, :], lift[i], sigm[i], ALU.mult),
                                     waits=[glu, lifted, inner_read.get(ex - 2)], signal=s_dve)
            for pair in range(2):
                for j in range(2):
                    t = 2 * pair + j
                    for f in range(halves):
                        done = pe.add(lambda e, t=t, j=j, f=f, ex=ex, pair=pair: e.matmul(
                            down_banks[pair][:, j * width:(j + 1) * width], inner[ex % 2][:, f, t * P:(t + 1) * P],
                            down_w[ex % 2][:, f, :], start=(f == 0), stop=(f == halves - 1)),
                            waits=[buffers[halves * ex + halves - 1], last_max, down_read.get((ex - 1, pair))],
                            signal=s_pe if (j, f) == (1, halves - 1) else None)
                for j in range(2):
                    t = 2 * pair + j
                    ffn_done = dve.add(lambda e, t=t, j=j, ex=ex, pair=pair: e.scalar_tensor_tensor(
                        out=ffn[:, t, :], in0=down_banks[pair][:, j * width:(j + 1) * width],
                        scalar=coef[:, t, ex:ex + 1], in1=ffn[:, t, :], op0=ALU.mult, op1=ALU.add),
                        waits=[done, ffn_done], signal=s_dve)
                down_read[ex, pair] = ffn_done
            inner_read[ex] = done
            if ex + 2 < experts:
                expert_loaded[ex + 2] = load_expert(ex + 2, [done])
        ln = norm_rstd(norm_stats(ffn, ffn_done))
        done = norm_apply(x1_t.rearrange("p h (t c) -> p (h t) c", c=width), ffn, ln)
        last = sp.add(lambda e: e.dma_start(out[0].rearrange("(t p) c -> p t c", p=P), x1_t.rearrange("p h (t c) -> p (h t) c", c=width)),
                      waits=[done], signal=s_out, by=16)

        block = ctx.enter_context(nc.Block())

        @block.sync
        def _(engine):
            sp.run(engine)
            engine.wait_ge(last[0].semaphore, last[1])

        @block.gpsimd
        def _(engine):
            pool.run(engine)

        @block.scalar
        def _(engine):
            act.run(engine)

        @block.tensor
        def _(engine):
            pe.run(engine)

        @block.vector
        def _(engine):
            dve.run(engine)


NAMES = ["L0_attn_x", "L0_attn_W_attn", "L0_attn_b_attn", "L0_attn_W_k2", "L0_attn_b_k2", "L0_attn_W_proj",
         "L0_attn_b_proj", "L0_ffn_router_indices", "L0_ffn_routing_weights", "L0_ffn_gate_up_proj",
         "L0_ffn_gate_up_proj_bias", "L0_ffn_down_proj", "L0_ffn_down_proj_bias"]


def kernel(**inputs):
    import concourse.bacc as bacc
    from concourse.bass_utils import run_bass_kernel_spmd

    nc = bacc.Bacc("TRN2", target_bir_lowering=False, num_devices=1)
    arrays, args = {}, []
    for name in NAMES:
        a = np.ascontiguousarray(inputs[name])
        arrays[name] = a
        args.append(nc.dram_tensor(name, a.shape, mybir.dt.from_np(a.dtype), kind="ExternalInput").ap())
    shape = arrays["L0_attn_x"].shape
    args.append(nc.dram_tensor("layer_out", shape, F32, kind="ExternalOutput").ap())
    build_layer(nc, *args)
    result = run_bass_kernel_spmd(nc, [arrays], core_ids=[0])
    return result.results[0]["layer_out"]
```

```python
from contextlib import ExitStack

import numpy as np

import concourse.bass as bass
from concourse import mybir

F32 = mybir.dt.float32
BF16 = mybir.dt.bfloat16
I32 = mybir.dt.int32
ALU = mybir.AluOpType
ACT = mybir.ActivationFunctionType

P = 128
HEADS, HEAD_DIM = 16, 16
GROUP = 4
GROUPS = HEADS // GROUP
UNITS = 2 * GROUPS
SLOTS = 10
LEAD = 7
PARTS_Q = (0, 0, 1, 0, 2, 1)
PARTS_K = (0, 1, 0, 2, 0, 1)
TERMS = len(PARTS_Q)
SCORE_ROWS = TERMS * HEAD_DIM
MAX_PARTS = 3
MASKED = -1e30
LN_EPS = 1e-5
SWIGLU_ALPHA, LIMIT = 1.702, 7.0

KEY_BANKS = [[(h, 0, 0)] for h in range(4)] + [[(h, 3, 0), (h, 1, 128)] for h in range(4)] + [
    [(0, 2, 0), (1, 2, 256)], [(2, 2, 0), (3, 2, 256)]]
BANK_OF = {(h, kb): (n, col) for n, parts in enumerate(KEY_BANKS) for h, kb, col in parts}
MAX_BANKS = [[(h, 3, 0)] for h in range(4)] + [[(h, 2, 0), (h, 0, 384)] for h in range(4)] + [
    [(0, 1, 0), (1, 1, 256)], [(2, 1, 0), (3, 1, 256)]]
TRIANGLES = [(512, 2, 1), (512, 2, 1), (512, 2, 2), (512, 2, 2), (256, 4, 1)]


class Signal:

    def __init__(self, semaphore):
        self.semaphore, self.count = semaphore, 0


class Queue:

    def __init__(self):
        self.steps, self.waited = [], {}

    def add(self, make, waits=(), signal=None, by=1):
        fresh = []
        for point in waits:
            if point is None:
                continue
            sig, value = point
            if self.waited.get(id(sig), 0) < value:
                self.waited[id(sig)] = value
                fresh.append((sig.semaphore, value))
        self.steps.append((make, fresh, signal.semaphore if signal else None, by))
        if signal:
            signal.count += by
            return signal, signal.count
        return None

    def run(self, engine):
        for make, waits, semaphore, by in self.steps:
            for s, value in waits:
                engine.wait_ge(s, value)
            done = make(engine)
            if semaphore is not None:
                done.then_inc(semaphore, by)


def build_layer(nc, x, w_attn, b_attn, w_k2, b_k2, w_proj, b_proj,
                router_indices, routing_weights, w_up, b_up, w_down, b_down, out):
    batches, tokens, width = x.shape
    blocks = tokens // P
    halves = width // P
    heads_half = HEADS // halves
    experts, _, inter2 = w_up.shape
    inter = inter2 // 2
    routed = router_indices.shape[0]
    assert (tokens, width) == (512, 256) and routed == tokens and inter == width
    end_of_units = UNITS * batches

    ctx = ExitStack()
    with ctx:
        def sb(name, shape, dt=F32):
            return ctx.enter_context(nc.sbuf_tensor(name, shape, dt))

        def ps(name, cols):
            return ctx.enter_context(nc.psum_tensor(name, [P, cols], F32))

        def signal(name):
            return Signal(ctx.enter_context(nc.semaphore(name)))

        ident = sb("ident", [P, P])
        wq = sb("wq", [P, halves, 2 * halves, P])
        wk2 = sb("wk2", [P, halves, halves, P])
        wp = sb("wp", [P, halves, width])
        bias_qk = sb("bias_qk", [P, 3 * halves])
        bias2 = sb("bias2", [P, width])
        stack_q = [sb(f"stack_q{i}", [P, HEADS, tokens], BF16) for i in range(2)]
        stack_k = [sb(f"stack_k{i}", [P, HEADS, tokens], BF16) for i in range(2)]
        stack_k2 = [sb(f"stack_k2{i}", [P, HEADS, tokens], BF16) for i in range(2)]
        RING = 6
        KEY_DEPTH, MAX_DEPTH = 2, 3
        prob = [sb(f"prob{i}", [P, 1024]) for i in range(RING)]
        value1 = sb("value1", [P, blocks, HEADS, 32])
        value2 = sb("value2", [P, blocks, HEADS, 32])
        x_in = [sb(f"x_in{i}", [P, blocks, width]) for i in range(2)]
        x_next = sb("x_next", [P, blocks, width])
        resid = sb("resid", [P, blocks, width])
        y_sum = [sb(f"y_sum{i}", [P, blocks, width]) for i in range(2)]
        y_second = [sb(f"y_second{i}", [P, blocks, GROUP, HEAD_DIM]) for i in range(2)]
        y_t = sb("y_t", [P, halves, tokens])
        x_t = sb("x_t", [P, halves, tokens])
        heads_t = sb("heads_t", [P, tokens])
        part_h = [sb(f"part_h{i}", [P, tokens], BF16) for i in range(2)]
        part_m = [sb(f"part_m{i}", [P, tokens], BF16) for i in range(2)]
        part_l = [sb(f"part_l{i}", [P, tokens], BF16) for i in range(2)]
        part_r = [sb(f"part_r{i}", [P, tokens]) for i in range(2)]
        max_cols = [sb(f"max_cols{i}", [P, 2, HEADS, blocks]) for i in range(2)]
        neg_h = sb("neg_h", [64, P], BF16)
        neg_m = sb("neg_m", [64, P], BF16)
        neg_l = sb("neg_l", [64, P], BF16)
        neg_r = sb("neg_r", [64, P])
        mask_rows = [sb(f"mask_rows{i}", [P, tokens], BF16) for i in range(2)]
        mask_first = sb("mask_first", [P, P], BF16)
        JUNK = 2
        junk = [sb(f"junk{i}", [P, tokens], BF16) for i in range(JUNK)]
        den = sb("den", [P, blocks, GROUP])
        rden = sb("rden", [P, blocks, GROUP])
        stats = sb("stats", [P, blocks, 6])
        mean_var = sb("mean_var", [P, blocks, 2])
        var_eps = sb("var_eps", [P, blocks])
        log_var = sb("log_var", [P, blocks])
        rstd = sb("rstd", [P, 5, blocks])
        shift = sb("shift", [P, blocks])
        eps_col = sb("eps_col", [P, 1])
        x1_routed = sb("x1_routed", [P, blocks, width])

        score_t = [ps(f"score_t{i}", 512) for i in range(KEY_DEPTH)]
        score = [ps(f"score{i}", 512) for i in range(MAX_DEPTH)]
        out_t = ps("out_t", 512)
        misc = ps("misc", 512)
        turn = ps("turn", 512)

        s_loadw = signal("s_loadw")
        s_const = signal("s_const")
        s_consta = signal("s_consta")
        s_x = [signal(f"s_x{i}") for i in range(2)]
        s_next = signal("s_next")
        s_resid_in = signal("s_resid_in")
        s_stack = {(kind, hf): signal(f"s_stack_{kind}{hf}") for kind in ("q", "k", "k2") for hf in range(halves)}
        s_maxrow = [signal(f"s_maxrow{i}") for i in range(2)]
        s_out = signal("s_out")
        s_score_t = signal("s_score_t")
        s_score = signal("s_score")
        s_pv = signal("s_pv")
        s_pe = signal("s_pe")
        s_exp = signal("s_exp")
        s_act = signal("s_act")
        s_max = signal("s_max")
        s_dve = signal("s_dve")
        s_mask = signal("s_mask")
        s_pool = signal("s_pool")
        s_ffn_w = [signal(f"s_ffn_w{i}") for i in range(2)]
        s_ffn_in = signal("s_ffn_in")

        pe, act, dve, pool, sp = (Queue() for _ in range(5))

        raw_attn = prob[0][:, :].rearrange("p (h n) -> p h n", h=halves)
        raw_k2 = prob[1][:, 0:halves * width].rearrange("p (h n) -> p h n", h=halves)
        raw_bias = prob[2][:, 0:width]
        sp.add(lambda e: e.dma_start(raw_attn, w_attn.rearrange("(h p) n -> p h n", p=P)), signal=s_loadw, by=16)
        sp.add(lambda e: e.dma_start(raw_k2, w_k2.rearrange("(h p) n -> p h n", p=P)), signal=s_loadw, by=16)
        sp.add(lambda e: e.dma_start(wp[:, :, :], w_proj.rearrange("(h p) n -> p h n", p=P)), signal=s_loadw, by=16)
        sp.add(lambda e: e.dma_start(raw_bias, b_proj.rearrange("(o n) -> o n", o=1).to_broadcast([P, width])),
               signal=s_loadw, by=16)
        bias_rows = prob[3][0:3 * halves, 0:P]
        bias_sorted = prob[3][0:3 * halves, P:2 * P]
        sp.add(lambda e: e.dma_start(prob[3][0:2 * halves, 0:P], b_attn.rearrange("(r p) -> r p", p=P)), signal=s_loadw, by=16)
        sp.add(lambda e: e.dma_start(prob[3][2 * halves:3 * halves, 0:P], b_k2.rearrange("(r p) -> r p", p=P)), signal=s_loadw, by=16)
        weights_loaded = (s_loadw, s_loadw.count)

        pool.add(lambda e: e.memset(ident[:, :], 1.0), signal=s_const)
        made = pool.add(lambda e: e.memset(x_next[:, :, :], 0.0), signal=s_const)
        next_zeroed = made
        pool.add(lambda e: e.memset(value1[:, :, :, :], 1.0), signal=s_const)
        pool.add(lambda e: e.memset(value2[:, :, :, :], 1.0), signal=s_const)
        for tile in (mask_rows[0], mask_rows[1], mask_first):
            pool.add(lambda e, tile=tile: e.memset(tile[:, :], 0.0), signal=s_const)
        made = pool.add(lambda e: e.memset(eps_col[:, :], LN_EPS), signal=s_const)
        pool.add(lambda e: e.affine_select(out=ident[:, :], in_=ident[:, :], compare_op=ALU.is_equal, fill=0.0,
                                           base=0, pattern=[[1, P]], channel_multiplier=-1),
                 waits=[made], signal=s_const)
        for a in range(2):
            tri = mask_rows[a][:, tokens - P:tokens]
            pool.add(lambda e, tri=tri, a=a: e.affine_select(
                out=tri, in_=tri, compare_op=ALU.is_ge, fill=MASKED, base=-a, pattern=[[-1, P]],
                channel_multiplier=1), signal=s_const)
        made = pool.add(lambda e: e.affine_select(
            out=mask_first[:, :], in_=mask_first[:, :], compare_op=ALU.is_ge, fill=MASKED, base=-1,
            pattern=[[-1, P]], channel_multiplier=1), signal=s_const)
        constants = made

        R = SCORE_ROWS
        for i in range(2):
            dve.add(lambda e, i=i: e.memset(stack_k2[i][R:R + 2 * MAX_PARTS, :, :], 1.0), signal=s_consta)
            rows_made = dve.add(lambda e, i=i: e.memset(stack_k[i][R:R + MAX_PARTS, :, :], 1.0), signal=s_consta)
        for i in range(2):
            rows_made = dve.add(lambda e, i=i: e.memset(stack_k2[i][R:R + MAX_PARTS, :, :], 0.0),
                            waits=[rows_made], signal=s_consta)
        dve.add(lambda e: e.memset(mask_first[0:1, 0:1], 0.0), waits=[constants], signal=s_consta)
        for piece in range(2 * halves):
            made = dve.add(lambda e, piece=piece: e.tensor_copy(
                wq[:, :, piece, :].rearrange("p c (d h) -> p c d h", d=HEAD_DIM),
                raw_attn[:, :, piece * P:(piece + 1) * P].rearrange("p c (h d) -> p c d h", d=HEAD_DIM)),
                waits=[weights_loaded], signal=s_consta)
        for hf in range(halves):
            made = dve.add(lambda e, hf=hf: e.tensor_copy(
                wk2[:, :, hf, :].rearrange("p c (d h) -> p c d h", d=HEAD_DIM),
                raw_k2[:, :, hf * P:(hf + 1) * P].rearrange("p c (h d) -> p c d h", d=HEAD_DIM)),
                signal=s_consta)
        dve.add(lambda e: e.tensor_tensor(bias2[:, :], raw_bias, raw_bias, ALU.add), signal=s_consta)
        made = dve.add(lambda e: e.tensor_copy(bias_sorted.rearrange("r (d h) -> r d h", d=HEAD_DIM),
                                               bias_rows.rearrange("r (h d) -> r d h", d=HEAD_DIM)), signal=s_consta)
        made = pe.add(lambda e: e.transpose(misc[:, 0:3 * halves], bias_sorted, ident[0:3 * halves, 0:3 * halves]),
                      waits=[made, constants], signal=s_pe)
        weights_ready = dve.add(lambda e: e.tensor_copy(bias_qk[:, :], misc[:, 0:3 * halves]), waits=[made], signal=s_consta)

        x_loaded, next_loaded, resid_loaded = {}, {}, {}
        x_t_ready = {}
        x_t_read = {}
        stack_ready = {}
        unit_scores_done = {}
        unit_max_done = {}
        unit_max_scores = {}
        max_rows_ready = {}
        exp_done, mask_done = {}, {}
        pair_read = {}
        bank_max = {}
        unit_pv_done = {}
        heads_copied = {}
        value1_ready, value2_ready = {}, {}
        y_added = {}
        state = {"misc_read": [weights_ready, constants], "turn_read": [constants], "junk": [None] * JUNK, "piece": 0, "heads_read": None,
                 "max_copied": None, "neg_sent": None, "den": None, "y_t_read": None,
                 "resid_free": None, "value1_free": None, "x_free": {}, "next_free": next_zeroed,
                 "neg_r": None}
        piece_history = []

        later = {}

        def put_off(slots, steps):
            later.setdefault(state["now"] + slots, []).append(steps)

        def run_put_off(now):
            for steps in later.pop(now, []):
                steps()

        def unit_parts(unit):
            return unit // UNITS, unit % UNITS // GROUPS, unit % GROUPS

        def load_x(b):
            x_loaded[b] = sp.add(lambda e: e.dma_start(x_in[b % 2][:, :, :], x[b].rearrange("(t p) c -> p t c", p=P)),
                                 waits=[state["x_free"].get(b)], signal=s_x[b % 2], by=16)

        def load_next(b):
            last = blocks - 1
            sp.add(lambda e: e.dma_start(x_next[:, 0:last, :], x[b, 1:1 + last * P, :].rearrange("(t p) c -> p t c", p=P)),
                   waits=[state["next_free"]], signal=s_next, by=16)
            next_loaded[b] = sp.add(lambda e: e.dma_start(x_next[0:P - 1, last, :], x[b, 1 + last * P:tokens, :]),
                                    signal=s_next, by=16)

        def load_resid(b):
            resid_loaded[b] = sp.add(lambda e: e.dma_start(resid[:, :, :], x[b].rearrange("(t p) c -> p t c", p=P)),
                                     waits=[state["resid_free"]], signal=s_resid_in, by=16)

        def transpose_x(b, hf):
            src = x_in[b % 2]
            for t in range(blocks):
                done = pe.add(lambda e, t=t: e.transpose(misc[:, t * P:(t + 1) * P], src[:, t, hf * P:(hf + 1) * P], ident[:, :]),
                              waits=[x_loaded[b]] + state["misc_read"], signal=s_pe if t == blocks - 1 else None)
            state["misc_read"] = []

            def copy_step():
                x_t_ready[b] = act.add(lambda e: e.activation(x_t[:, hf, :], misc[:, :], ACT.Copy),
                                       waits=[done, x_t_read.get(b - 1)], signal=s_act)
                state["misc_read"] = [x_t_ready[b]]

            put_off(1, copy_step)

        def project_piece(kind, b, hf, c):
            n = state["piece"]
            i = n % 2
            old = piece_history[n - 2] if n >= 2 else {}
            piece = {"q": hf, "k": halves + hf, "k2": 2 * halves + hf}[kind]
            w = wk2[:, c, hf, :] if kind == "k2" else wq[:, c, piece, :]
            done = pe.add(lambda e: e.matmul(misc[:, :], w, x_t[:, c, :], start=(c == 0), stop=(c == halves - 1)),
                          waits=[x_t_ready[b], weights_ready] + state["misc_read"],
                          signal=s_pe if c == halves - 1 else None)
            if c < halves - 1:
                return
            state["piece"] += 1
            x_t_read[b] = done
            bias = bias_qk[:, piece:piece + 1]
            high = act.add(lambda e: e.activation(part_h[i][:, :], misc[:, :], ACT.Identity, bias=bias),
                           waits=[done, weights_ready, old.get("sent")], signal=s_act)
            record = {"parts": (part_h[i], part_m[i], part_l[i])}
            piece_history.append(record)
            state["misc_read"] = []

            def rest_step():
                record["rest"] = dve.add(lambda e: e.scalar_tensor_tensor(
                    out=part_r[i][:, :], in0=misc[:, :], scalar=bias, in1=part_h[i][:, :], op0=ALU.add,
                    op1=ALU.subtract), waits=[high, old.get("low")], signal=s_dve)
                state["misc_read"] = [record["rest"]]

            def low_steps():
                middle = act.add(lambda e: e.activation(part_m[i][:, :], part_r[i][:, :], ACT.Copy),
                                 waits=[record["rest"], old.get("sent")], signal=s_act)
                record["low"] = pool.add(lambda e: e.tensor_tensor(part_l[i][:, :], part_r[i][:, :], part_m[i][:, :], ALU.subtract),
                                         waits=[middle, old.get("sent")], signal=s_pool)

            put_off(1, rest_step)
            put_off(5, low_steps)
            put_off(6, lambda: send_piece(kind, b, hf, record))

        def send_piece(kind, b, hf, record):
            stack = {"q": stack_q, "k": stack_k, "k2": stack_k2}[kind][b % 2]
            last_group = (hf + 1) * GROUPS // halves - 1
            reader = UNITS * (b - 2) + (0 if kind == "k" else GROUPS) + last_group
            free = unit_scores_done.get(reader)
            for term, part in enumerate(PARTS_Q if kind == "q" else PARTS_K):
                sent = sp.add(lambda e, term=term, part=part: e.dma_start(
                    stack[term * HEAD_DIM:(term + 1) * HEAD_DIM, hf * heads_half:(hf + 1) * heads_half, :],
                    record["parts"][part][:, :]), waits=[record["low"], free, constants], signal=s_stack[kind, hf], by=16)
            stack_ready[kind, b, hf] = record["sent"] = sent

        def stacks(unit):
            b, a, g = unit_parts(unit)
            kind = "k2" if a else "k"
            keys = (stack_k2 if a else stack_k)[b % 2]
            hf = g * halves // GROUPS
            return stack_q[b % 2], keys, [stack_ready["q", b, hf], stack_ready[kind, b, hf]]

        def max_bank(unit, n):
            b, a, g = unit_parts(unit)
            queries, keys, ready = stacks(unit)
            number = len(MAX_BANKS) * unit + n
            bank = score[number % MAX_DEPTH]
            for h, qb, col in MAX_BANKS[n]:
                head, keys_n = GROUP * g + h, P * (qb + 1)
                last = (h, qb, col) == MAX_BANKS[n][-1]
                done = pe.add(lambda e, head=head, qb=qb, col=col, keys_n=keys_n: e.matmul(
                    bank[:, col:col + keys_n], queries[0:SCORE_ROWS, head, qb * P:(qb + 1) * P],
                    keys[0:SCORE_ROWS, head, 0:keys_n], start=True, stop=True),
                    waits=ready + [bank_max.get(number - MAX_DEPTH)], signal=s_score if last else None)
            unit_max_scores[unit] = done
            for h, qb, col in MAX_BANKS[n]:
                head, keys_n = GROUP * g + h, P * (qb + 1)
                mask = mask_first[:, :] if a and qb == 0 else mask_rows[a][:, tokens - keys_n:tokens]
                k = s_max.count % JUNK
                target = max_cols[b % 2]
                state["junk"][k] = bank_max[number] = dve.add(
                    lambda e, head=head, qb=qb, col=col, keys_n=keys_n, mask=mask, k=k: e.tensor_tensor_reduce(
                        junk[k][:, 0:keys_n], bank[:, col:col + keys_n], mask, 1.0, -3e38, ALU.add, ALU.max,
                        target[:, a, head, qb:qb + 1]),
                    waits=[done, constants, state["junk"][k]], signal=s_max)
            unit_max_done[unit] = bank_max[number]

        def negate_maxima(b, a):
            src = max_cols[b % 2][:, a, :, :].rearrange("p h q -> p (h q)")
            n = HEADS * blocks
            done = pe.add(lambda e: e.transpose(turn[0:n, 0:P], src, ident[:, :]),
                          waits=[unit_max_done[UNITS * b + GROUPS * a + GROUPS - 1]] + state["turn_read"], signal=s_pe)
            high = act.add(lambda e: e.activation(neg_h[:, :], turn[0:n, 0:P], ACT.Copy, scale=-1.0),
                           waits=[done, state["neg_sent"]], signal=s_act)
            state["turn_read"] = []
            made = {}

            def rest_step():
                made["rest"] = dve.add(lambda e: e.scalar_tensor_tensor(
                    out=neg_r[:, :], in0=turn[0:n, 0:P], scalar=-1.0, in1=neg_h[:, :], op0=ALU.mult,
                    op1=ALU.subtract), waits=[high, state["neg_r"]], signal=s_dve)
                state["turn_read"] = [made["rest"]]

            def low_steps():
                middle = act.add(lambda e: e.activation(neg_m[:, :], neg_r[:, :], ACT.Copy),
                                 waits=[made["rest"], state["neg_sent"]], signal=s_act)
                low = pool.add(lambda e: e.tensor_tensor(neg_l[:, :], neg_r[:, :], neg_m[:, :], ALU.subtract),
                               waits=[middle, state["neg_sent"]], signal=s_pool)
                state["neg_r"] = low
                free = unit_scores_done.get(UNITS * (b - 2) + UNITS - 1)
                for part, tile in enumerate((neg_h, neg_m, neg_l)):
                    row = SCORE_ROWS + MAX_PARTS * a + part
                    sent = sp.add(lambda e, row=row, tile=tile: e.dma_start(stack_q[b % 2][row:row + 1, :, :], tile[:, :]),
                                  waits=[low, free], signal=s_maxrow[a], by=16)
                max_rows_ready[b, a] = state["neg_sent"] = sent

            put_off(1, rest_step)
            put_off(5, low_steps)

        def key_bank(unit, n):
            b, a, g = unit_parts(unit)
            queries, keys, ready = stacks(unit)
            number = SLOTS * unit + n
            pair = number // 2
            bank = score_t[number % KEY_DEPTH]
            rows = SCORE_ROWS + MAX_PARTS * (a + 1)
            ready = ready + [max_rows_ready[b, 0], max_rows_ready[b, a]]
            for h, kb, col in KEY_BANKS[n]:
                head, queries_n = GROUP * g + h, tokens - P * kb
                last = (h, kb, col) == KEY_BANKS[n][-1]
                done = pe.add(lambda e, head=head, kb=kb, col=col, queries_n=queries_n: e.matmul(
                    bank[:, col:col + queries_n], keys[0:rows, head, kb * P:(kb + 1) * P],
                    queries[0:rows, head, kb * P:tokens], start=True, stop=True),
                    waits=ready + [exp_done.get(number - KEY_DEPTH)], signal=s_score_t if last else None)
            unit_scores_done[unit] = done
            tile = prob[pair % RING]
            exp_done[number] = act.add(
                lambda e: e.activation(tile[:, n % 2 * 512:n % 2 * 512 + 512], bank[:, :], ACT.Exp,
                                       scale=1.0 / np.sqrt(HEAD_DIM).item()),
                waits=[done, pair_read.get(pair - RING), weights_ready], signal=s_exp)
            if n % 2 == 0:
                return
            step, runs, cut = TRIANGLES[n // 2]
            view = tile[:, :].rearrange("p (r s) -> p r s", s=step)[:, :, 0:cut * P]
            pattern = [[0, runs], [0, cut], [1, P]]
            mask_done[pair] = pool.add(lambda e: e.affine_select(
                out=view, in_=view, compare_op=ALU.is_ge, fill=0.0, base=-a, pattern=pattern,
                channel_multiplier=-1), waits=[exp_done[number]], signal=s_mask)

        def weigh(unit, kb, first, count, start=False, stop=False):
            b, a, g = unit_parts(unit)
            value = value2 if a else value1
            ready = value2_ready[b, g] if a else value1_ready[b]
            for h in range(GROUP):
                n, col = BANK_OF[h, kb]
                pair = (SLOTS * unit + n) // 2
                at = n % 2 * 512 + col + first - P * kb
                done = pe.add(lambda e, h=h, pair=pair, at=at: e.matmul(
                    out_t[32 * h:32 * h + 32, first:first + count], value[:, kb, GROUP * g + h, :],
                    prob[pair % RING][:, at:at + count], start=start, stop=stop, skip_group_check=True),
                    waits=[mask_done[pair], ready, heads_copied.get(unit - 1)],
                    signal=s_pv if h == GROUP - 1 else None)
            return done

        def weigh_slot(slot, unit):
            pair = SLOTS // 2 * unit
            if slot == 6 and 0 <= unit < end_of_units:
                weigh(unit, 0, 0, 2 * P, start=True)
            if slot == 9 and 0 <= unit < end_of_units:
                pair_read[pair] = pair_read[pair + 1] = weigh(unit, 0, 2 * P, 2 * P)
            before = unit - 1
            if not 0 <= before < end_of_units:
                return
            pair = SLOTS // 2 * before
            if slot == 0:
                weigh(before, 1, P, 3 * P)
            if slot == 2:
                pair_read[pair + 2] = pair_read[pair + 3] = weigh(before, 3, 3 * P, P)
                pair_read[pair + 4] = unit_pv_done[before] = weigh(before, 2, 2 * P, 2 * P, stop=True)
                put_off(1, lambda: copy_heads(before))

        def copy_heads(unit):
            heads_copied[unit] = act.add(lambda e: e.activation(heads_t[:, :], out_t[:, :], ACT.Copy),
                                         waits=[unit_pv_done[unit], state["heads_read"]], signal=s_act)

        def finish_unit(unit):
            b, a, g = unit_parts(unit)
            for t in range(blocks):
                done = pe.add(lambda e, t=t: e.transpose(turn[:, t * P:(t + 1) * P], heads_t[:, t * P:(t + 1) * P], ident[:, :]),
                              waits=[heads_copied[unit]] + state["turn_read"], signal=s_pe if t == blocks - 1 else None)
            state["heads_read"] = done
            heads = turn[:, :].rearrange("p (t h w) -> p t h w", t=blocks, h=GROUP)
            chans = slice(g * GROUP * HEAD_DIM, (g + 1) * GROUP * HEAD_DIM)
            y = y_sum[b % 2][:, :, chans].rearrange("p t (h d) -> p t h d", d=HEAD_DIM)
            second = y_second[g % 2][:, :, :, :]
            made = {}

            def normalise():
                sums, ready = heads[:, :, :, HEAD_DIM], done
                if a:
                    ready = dve.add(lambda e: e.tensor_scalar(den[:, :, :], sums, 1e-30, None, ALU.max),
                                    waits=[done, state["den"]], signal=s_dve)
                inverse = dve.add(lambda e: e.reciprocal(rden[:, :, :], den[:, :, :] if a else sums),
                                  waits=[ready, state["den"]], signal=s_dve)
                wide = bass.AP(rden[:, :, :].tensor, rden[:, :, :].offset,
                               [list(rden[:, :, :].ap[0]), [GROUP, blocks], [1, GROUP], [0, HEAD_DIM]])
                made["normal"] = dve.add(
                    lambda e: e.tensor_tensor(second if a else y, heads[:, :, :, 0:HEAD_DIM], wide, ALU.mult),
                    waits=[inverse, state.get(("second", g % 2)) if a else state.get(("y_t", b - 2))], signal=s_dve)
                state["den"] = made["normal"]
                state["turn_read"] = [made["normal"]]

            def add_up():
                if a:
                    y_added[b] = state["second", g % 2] = pool.add(
                        lambda e: e.tensor_tensor(y, y, second, ALU.add),
                        waits=[made["normal"], value2_ready[b, g]], signal=s_pool)
                    return
                nxt = x_next[:, :, chans].rearrange("p t (h d) -> p t h d", d=HEAD_DIM)
                value2_ready[b, g] = state["next_free"] = pool.add(lambda e: e.tensor_tensor(
                    value2[:, :, GROUP * g:GROUP * g + GROUP, 0:HEAD_DIM], nxt, y, ALU.subtract),
                    waits=[made["normal"], next_loaded[b], constants, unit_pv_done.get(UNITS * (b - 1) + GROUPS + g)],
                    signal=s_pool)

            state["turn_read"] = []
            put_off(1, normalise)
            put_off(5, add_up)

        def transpose_y(b, hf):
            src = y_sum[b % 2]
            for t in range(blocks):
                done = pe.add(lambda e, t=t: e.transpose(misc[:, t * P:(t + 1) * P], src[:, t, hf * P:(hf + 1) * P], ident[:, :]),
                              waits=[y_added[b]] + state["misc_read"], signal=s_pe if t == blocks - 1 else None)
            state["y_t", b] = done
            state["misc_read"] = []

            def copy_step():
                state["y_t_ready"] = act.add(lambda e: e.activation(y_t[:, hf, :], misc[:, :], ACT.Copy),
                                             waits=[done, state["y_t_read"]], signal=s_act)
                state["misc_read"] = [state["y_t_ready"]]

            put_off(1, copy_step)

        def project_out(b, pair, j):
            t = 2 * pair + j
            for c in range(halves):
                done = pe.add(lambda e, c=c: e.matmul(
                    misc[:, j * width:(j + 1) * width], y_t[:, c, t * P:(t + 1) * P], wp[:, c, :],
                    start=(c == 0), stop=(c == halves - 1)),
                    waits=[state["y_t_ready"], weights_loaded] + state["misc_read"],
                    signal=s_pe if (j, c) == (1, halves - 1) else None)
            if j == 0:
                return
            state["y_t_read"] = done
            rows = resid[:, 2 * pair:2 * pair + 2, :]
            state["misc_read"] = []

            def add_step():
                state["attended"] = dve.add(lambda e: e.tensor_tensor(
                    rows, misc[:, :].rearrange("p (t c) -> p t c", t=2), rows, ALU.add),
                    waits=[done, state["biased"]], signal=s_dve)
                state["misc_read"] = [state["attended"]]

            put_off(1, add_step)

        def add_bias(b):
            wide = bass.AP(bias2[:, :].tensor, bias2[:, :].offset, [list(bias2[:, :].ap[0]), [0, blocks], [1, width]])
            state["biased"] = pool.add(lambda e: e.tensor_tensor(resid[:, :, :], resid[:, :, :], wide, ALU.add),
                                       waits=[resid_loaded[b], weights_ready], signal=s_pool)

        def variance_eps(aggregated):
            return pool.add(lambda e: e.tensor_scalar(var_eps[:, :], mean_var[:, :, 1], LN_EPS, None, ALU.add),
                            waits=[aggregated], signal=s_pool)

        def guess_rstd(v):
            log = act.add(lambda e: e.activation(log_var[:, :], var_eps[:, :], ACT.Ln), waits=[v], signal=s_act)
            return act.add(lambda e: e.activation(rstd[:, 0, :], log_var[:, :], ACT.Exp, scale=-0.5),
                           waits=[log, state.get("shifted")], signal=s_act)

        def refine_rstd(guess):
            s = pool.add(lambda e: e.tensor_tensor(rstd[:, 1, :], rstd[:, 0, :], rstd[:, 0, :], ALU.mult),
                         waits=[guess], signal=s_pool)
            s = pool.add(lambda e: e.tensor_tensor(rstd[:, 2, :], rstd[:, 1, :], var_eps[:, :], ALU.mult),
                         waits=[s], signal=s_pool)
            s = pool.add(lambda e: e.tensor_scalar(rstd[:, 3, :], rstd[:, 2, :], -0.5, 1.5, ALU.mult, ALU.add),
                         waits=[s], signal=s_pool)
            s = pool.add(lambda e: e.tensor_tensor(rstd[:, 4, :], rstd[:, 3, :], rstd[:, 0, :], ALU.mult),
                         waits=[s, state.get("applied")], signal=s_pool)
            s = pool.add(lambda e: e.tensor_tensor(log_var[:, :], mean_var[:, :, 0], rstd[:, 4, :], ALU.mult),
                         waits=[s], signal=s_pool)
            s = pool.add(lambda e: e.tensor_scalar(shift[:, :], log_var[:, :], -1.0, None, ALU.mult),
                         waits=[s], signal=s_pool)
            state["shifted"] = s
            return s

        def apply_block(dst, src, t, ready):
            state["applied"] = act.add(lambda e: e.activation(dst[:, t, :], src[:, t, :], ACT.Identity,
                                                              bias=shift[:, t:t + 1], scale=rstd[:, 4, t:t + 1]),
                                       waits=[ready], signal=s_act)
            return state["applied"]

        def layer_norm(dst, src, ready, after):
            made = {}

            def stats_step(t):
                made["s", t] = dve.add(lambda e: e.bn_stats(stats[:, t, :], src[:, t, :]),
                                       waits=[ready(), state.get("aggregated")], signal=s_dve)

            def aggregate():
                for t in range(blocks):
                    done = dve.add(lambda e, t=t: e.bn_aggr(mean_var[:, t, :], stats[:, t, :]),
                                   waits=[made["s", blocks - 1], state.get("shifted")], signal=s_dve)
                state["aggregated"] = done

            for t in range(blocks):
                put_off(1 + t, lambda t=t: stats_step(t))
            put_off(1 + blocks, aggregate)
            put_off(5 + blocks, lambda: made.update(v=variance_eps(state["aggregated"])))
            put_off(6 + blocks, lambda: made.update(g=guess_rstd(made["v"])))
            put_off(7 + blocks, lambda: made.update(r=refine_rstd(made["g"])))

            def apply_step(t):
                made["a"] = apply_block(dst, src, t, made["r"])

            for t in range(blocks):
                put_off(9 + blocks + t, lambda t=t: apply_step(t))
            put_off(9 + 2 * blocks, lambda: after(made["a"]))

        def store(b, ready):
            state["resid_free"] = sp.add(lambda e: e.dma_start(out[b].rearrange("(t p) c -> p t c", p=P), resid[:, :, :]),
                                         waits=[ready], signal=s_out, by=16)

        def extra(unit, slot):
            place = unit % UNITS
            ahead = (unit - place) // UNITS
            pieces = {4: ("k", 0), 5: ("q", 0), 6: ("k", 1), 7: ("q", 1), 0: ("k2", 0), 1: ("k2", 1)}
            if slot in (7, 8) and place in pieces:
                b = ahead + (2 if place >= 4 else 1)
                if 0 <= b < batches:
                    project_piece(pieces[place][0], b, pieces[place][1], slot - 7)
            if (place, slot) in ((3, 8), (4, 1)) and 0 <= ahead + 2 < batches:
                transpose_x(ahead + 2, place - 3)
            if slot == 0 and place == 6 and 0 <= ahead + 1 < batches:
                negate_maxima(ahead + 1, 0)
            if slot == 0 and place == 2 and 0 <= ahead < batches:
                negate_maxima(ahead, 1)
            if place == 5 and slot == 3 and 0 <= ahead + 1 < batches:
                b = ahead + 1
                value1_ready[b] = dve.add(lambda e: e.tensor_copy(
                    value1[:, :, :, 0:HEAD_DIM], x_in[b % 2][:, :, :].rearrange("p t (h d) -> p t h d", d=HEAD_DIM)),
                    waits=[x_loaded[b], constants, unit_pv_done.get(UNITS * (b - 1) + GROUPS - 1)], signal=s_dve)
                state["x_free"][b + 2] = value1_ready[b]
                load_next(b)
                if b + 2 < batches:
                    load_x(b + 2)
            b = ahead - 1
            if not 0 <= b < batches:
                return
            if (place, slot) == (0, 0):
                load_resid(b)
            if (place, slot) == (1, 5):
                add_bias(b)
            if (place, slot) in ((1, 3), (2, 3)):
                transpose_y(b, place - 1)
            if (place, slot) in ((2, 7), (2, 8), (3, 3), (3, 4)):
                project_out(b, place - 2, slot - 7 if place == 2 else slot - 3)
            if (place, slot) == (3, 5):
                if b == 0:
                    def keep(done):
                        state["resid_free"] = state["x1_routed"] = done
                    layer_norm(x1_routed, resid, lambda: state["attended"], keep)
                else:
                    layer_norm(resid, resid, lambda: state["attended"], lambda done: layer_norm(
                        resid, resid, lambda: done, lambda done: store(b, done)))

        act.add(lambda e: e.preload_act_table_set("natural_log_exp_and_others") or None)
        load_x(0)
        if batches > 1:
            load_x(1)
        for unit in range(-2 * UNITS + 2, end_of_units + UNITS):
            for slot in range(SLOTS):
                if 0 <= unit < end_of_units:
                    key_bank(unit, slot)
                if 0 <= unit + LEAD < end_of_units:
                    max_bank(unit + LEAD, slot)
                state["now"] = SLOTS * unit + slot
                weigh_slot(slot, unit)
                if slot == 5 and 0 <= unit - 1 < end_of_units:
                    finish_unit(unit - 1)
                extra(unit, slot)
                run_put_off(state["now"])
        while later:
            state["now"] = min(later)
            run_put_off(state["now"])

        free = unit_scores_done[end_of_units - 1]

        def in_stack(stack, first, shape):
            n = int(np.prod(shape))
            flat = stack[:, :, :].rearrange("p h t -> p (h t)")[:, 2 * first:2 * (first + n)].bitcast(F32)
            names = "abcd"[:len(shape)]
            sizes = dict(zip(names, shape))
            return flat.rearrange(f"p ({' '.join(names)}) -> p {' '.join(names)}", **sizes)

        up_w = [in_stack(stack_k[i], 0, (halves, inter2)) for i in range(2)]
        down_w = [in_stack(stack_k[i], halves * inter2, (halves, width)) for i in range(2)]
        x1_t = in_stack(stack_q[0], 0, (halves, tokens))
        gate = [in_stack(stack_q[0], (2 + i) * 512, (tokens,)) for i in range(2)]
        sigm = [in_stack(stack_q[0], (4 + i) * 512, (tokens,)) for i in range(2)]
        lift = [in_stack(stack_q[0], (6 + i) * 512, (tokens,)) for i in range(2)]
        inner = [in_stack(stack_q[1], 1024 * i, (halves, tokens)) for i in range(2)]
        ffn = in_stack(stack_q[1], 2048, (blocks, width))
        down_b = in_stack(stack_k2[0], 0, (width,))
        up_b = in_stack(stack_k2[0], 256, (experts * inter2 // P,))
        chosen = in_stack(stack_k2[0], 512, (blocks, 2))
        same = in_stack(stack_k2[0], 528, (blocks, 2))
        route = in_stack(stack_k2[0], 544, (blocks, experts))
        coef = in_stack(stack_k2[0], 576, (blocks, experts))
        coef_t = in_stack(stack_k2[0], 1024, (tokens,))
        up_b_rows = in_stack(stack_k2[0], 1536, (P,))
        chosen_i = chosen_raw = in_stack(stack_k2[0], 1664, (blocks, 2)).bitcast(I32)

        def load_expert(ex, waits):
            i = ex % 2
            sp.add(lambda e: e.dma_start(up_w[i], w_up[ex].rearrange("(h p) n -> p h n", p=P)),
                   waits=waits, signal=s_ffn_w[i], by=16)
            return sp.add(lambda e: e.dma_start(down_w[i], w_down[ex].rearrange("(h p) n -> p h n", p=P)),
                          signal=s_ffn_w[i], by=16)

        n_rows = experts * inter2 // P
        sp.add(lambda e: e.dma_start(chosen_i, router_indices.rearrange("(t p) k -> p t k", p=P)),
               waits=[free], signal=s_ffn_in, by=16)
        sp.add(lambda e: e.dma_start(route, routing_weights.rearrange("(t p) k -> p t k", p=P)), signal=s_ffn_in, by=16)
        sp.add(lambda e: e.dma_start(down_b[0:experts, :], b_down), signal=s_ffn_in, by=16)
        ffn_loaded = sp.add(lambda e: e.dma_start(up_b_rows[0:n_rows, :], b_up.rearrange("x (r p) -> (x r) p", p=P)),
                            signal=s_ffn_in, by=16)
        expert_loaded = {ex: load_expert(ex, []) for ex in range(2)}

        step = dve.add(lambda e: e.tensor_copy(chosen, chosen_i), waits=[ffn_loaded, free], signal=s_dve)
        for ex in range(experts):
            step = dve.add(lambda e, ex=ex: e.tensor_scalar(same, chosen, float(ex), None, ALU.is_equal),
                           waits=[step], signal=s_dve)
            step = dve.add(lambda e, ex=ex: e.tensor_tensor(coef[:, :, ex], same[:, :, 0], same[:, :, 1], ALU.add),
                           waits=[step], signal=s_dve)
        coef_ready = dve.add(lambda e: e.tensor_tensor(coef, coef, route, ALU.mult), waits=[step], signal=s_dve)

        for hf in range(halves):
            for t in range(blocks):
                done = pe.add(lambda e, t=t, hf=hf: e.transpose(misc[:, t * P:(t + 1) * P], x1_routed[:, t, hf * P:(hf + 1) * P], ident[:, :]),
                              waits=[state["x1_routed"]] + state["misc_read"], signal=s_pe if t == blocks - 1 else None)
            x1_t_ready = act.add(lambda e, hf=hf: e.activation(x1_t[:, hf, :], misc[:, :], ACT.Copy), waits=[done, free], signal=s_act)
            state["misc_read"] = [x1_t_ready]
        gates_rows = up_b_rows[0:n_rows, :].rearrange("r (c two) -> r two c", two=2)
        for two in range(2):
            done = pe.add(lambda e, two=two: e.transpose(misc[0:64, two * n_rows:(two + 1) * n_rows], gates_rows[:, two, :], ident[0:n_rows, 0:n_rows]),
                          waits=[ffn_loaded] + state["misc_read"], signal=s_pe if two else None)
        bias_lo = act.add(lambda e: e.activation(up_b[0:64, :].rearrange("p (w x f) -> p w x f", w=2, x=experts),
                                                 misc[0:64, 0:2 * n_rows].rearrange("p (w x f two) -> p w x f two", w=2, x=experts, two=2)[:, :, :, :, 0],
                                                 ACT.Copy), waits=[done, free], signal=s_act)
        state["misc_read"] = [bias_lo]
        odd = in_stack(stack_k2[0], 1792, (n_rows,))
        odd_copy = act.add(lambda e: e.activation(odd[0:64, :].rearrange("p (w x f) -> p w x f", w=2, x=experts),
                                                  misc[0:64, 0:2 * n_rows].rearrange("p (w x f two) -> p w x f two", w=2, x=experts, two=2)[:, :, :, :, 1],
                                                  ACT.Copy), waits=[done], signal=s_act)
        state["misc_read"] = [odd_copy]
        up_b_ready = sp.add(lambda e: e.dma_start(up_b[64:128, :], odd[0:64, :]), waits=[odd_copy, bias_lo], signal=s_ffn_in, by=16)
        for t in range(blocks):
            done = pe.add(lambda e, t=t: e.transpose(misc[0:experts, t * P:(t + 1) * P], coef[:, t, :], ident[:, :]),
                          waits=[coef_ready] + state["misc_read"], signal=s_pe if t == blocks - 1 else None)
        coef_t_ready = act.add(lambda e: e.activation(coef_t[0:experts, :], misc[0:experts, :], ACT.Copy),
                               waits=[done, free], signal=s_act)
        state["misc_read"] = [coef_t_ready]
        ffn_done = None
        for pair in range(2):
            for j in range(2):
                t = 2 * pair + j
                done = pe.add(lambda e, t=t, j=j: e.matmul(misc[:, j * width:(j + 1) * width], coef_t[0:experts, t * P:(t + 1) * P],
                                                           down_b[0:experts, :], start=True, stop=True),
                              waits=[coef_t_ready] + state["misc_read"], signal=s_pe if j else None)
            rows = slice(2 * pair, 2 * pair + 2)
            ffn_done = dve.add(lambda e, rows=rows: e.tensor_tensor(
                ffn[:, rows, :], misc[:, :].rearrange("p (t c) -> p t c", t=2), x1_routed[:, rows, :], ALU.add),
                waits=[done, state["x1_routed"], free], signal=s_dve)
            state["misc_read"] = [ffn_done]

        gate_banks = [score_t[0][:, :], score_t[1][:, :]]
        up_banks = [turn[:, :], score[2][:, :]]
        down_banks = [score[0], score[1]]
        last_exp = exp_done[SLOTS * end_of_units - 1]
        last_max = unit_max_done[end_of_units - 1]
        bank_read, buffers, inner_read, down_read = {}, {}, {}, {}
        for ex in range(experts):
            w = up_w[ex % 2]
            for f in range(halves):
                n = halves * ex + f
                i = n % 2
                for two, bank in enumerate((gate_banks[i], up_banks[i])):
                    for c in range(halves):
                        done = pe.add(lambda e, w=w, c=c, f=f, two=two, bank=bank: e.matmul(
                            bank, w[:, c, 2 * P * f + two:2 * P * (f + 1):2], x1_t[:, c, :],
                            start=(c == 0), stop=(c == halves - 1)),
                            waits=[expert_loaded[ex], x1_t_ready, last_exp, last_max, bank_read.get(n - 2)],
                            signal=s_pe if (two, c) == (1, halves - 1) else None)
                bg = up_b[:, ex * halves + f:ex * halves + f + 1]
                bu = up_b[:, (experts + ex) * halves + f:(experts + ex) * halves + f + 1]
                old = buffers.get(n - 2)
                gated = dve.add(lambda e, i=i, bg=bg: e.tensor_scalar(gate[i], gate_banks[i], bg, LIMIT, ALU.add, ALU.min),
                                waits=[done, up_b_ready, old], signal=s_dve)
                lifted = dve.add(lambda e, i=i, bu=bu: e.tensor_scalar(lift[i], up_banks[i], bu, LIMIT, ALU.add, ALU.min),
                                 waits=[old], signal=s_dve)
                bank_read[n] = lifted
                sig = act.add(lambda e, i=i: e.activation(sigm[i], gate[i], ACT.Sigmoid, scale=SWIGLU_ALPHA),
                              waits=[gated, old], signal=s_act)
                lifted = dve.add(lambda e, i=i: e.tensor_scalar(lift[i], lift[i], -LIMIT, 1.0, ALU.max, ALU.add),
                                 waits=[lifted], signal=s_dve)
                glu = pool.add(lambda e, i=i: e.tensor_tensor(sigm[i], gate[i], sigm[i], ALU.mult), waits=[sig, gated], signal=s_pool)
                buffers[n] = dve.add(lambda e, i=i, ex=ex, f=f: e.tensor_tensor(inner[ex % 2][:, f, :], lift[i], sigm[i], ALU.mult),
                                     waits=[glu, lifted, inner_read.get(ex - 2)], signal=s_dve)
            for pair in range(2):
                for j in range(2):
                    t = 2 * pair + j
                    for f in range(halves):
                        done = pe.add(lambda e, t=t, j=j, f=f, ex=ex, pair=pair: e.matmul(
                            down_banks[pair][:, j * width:(j + 1) * width], inner[ex % 2][:, f, t * P:(t + 1) * P],
                            down_w[ex % 2][:, f, :], start=(f == 0), stop=(f == halves - 1)),
                            waits=[buffers[halves * ex + halves - 1], last_max, down_read.get((ex - 1, pair))],
                            signal=s_pe if (j, f) == (1, halves - 1) else None)
                for j in range(2):
                    t = 2 * pair + j
                    ffn_done = dve.add(lambda e, t=t, j=j, ex=ex, pair=pair: e.scalar_tensor_tensor(
                        out=ffn[:, t, :], in0=down_banks[pair][:, j * width:(j + 1) * width],
                        scalar=coef[:, t, ex:ex + 1], in1=ffn[:, t, :], op0=ALU.mult, op1=ALU.add),
                        waits=[done, ffn_done], signal=s_dve)
                down_read[ex, pair] = ffn_done
            inner_read[ex] = done
            if ex + 2 < experts:
                expert_loaded[ex + 2] = load_expert(ex + 2, [done])
        normed = {}
        layer_norm(x1_t.rearrange("p h (t c) -> p (h t) c", c=width), ffn, lambda: ffn_done,
                   lambda done: normed.update(done=done))
        while later:
            state["now"] = min(later)
            run_put_off(state["now"])
        done = normed["done"]
        last = sp.add(lambda e: e.dma_start(out[0].rearrange("(t p) c -> p t c", p=P), x1_t.rearrange("p h (t c) -> p (h t) c", c=width)),
                      waits=[done], signal=s_out, by=16)

        block = ctx.enter_context(nc.Block())

        @block.sync
        def _(engine):
            sp.run(engine)
            engine.wait_ge(last[0].semaphore, last[1])

        @block.gpsimd
        def _(engine):
            pool.run(engine)

        @block.scalar
        def _(engine):
            act.run(engine)

        @block.tensor
        def _(engine):
            pe.run(engine)

        @block.vector
        def _(engine):
            dve.run(engine)


NAMES = ["L0_attn_x", "L0_attn_W_attn", "L0_attn_b_attn", "L0_attn_W_k2", "L0_attn_b_k2", "L0_attn_W_proj",
         "L0_attn_b_proj", "L0_ffn_router_indices", "L0_ffn_routing_weights", "L0_ffn_gate_up_proj",
         "L0_ffn_gate_up_proj_bias", "L0_ffn_down_proj", "L0_ffn_down_proj_bias"]


def kernel(**inputs):
    import concourse.bacc as bacc
    from concourse.bass_utils import run_bass_kernel_spmd

    nc = bacc.Bacc("TRN2", target_bir_lowering=False, num_devices=1)
    arrays, args = {}, []
    for name in NAMES:
        a = np.ascontiguousarray(inputs[name])
        arrays[name] = a
        args.append(nc.dram_tensor(name, a.shape, mybir.dt.from_np(a.dtype), kind="ExternalInput").ap())
    shape = arrays["L0_attn_x"].shape
    args.append(nc.dram_tensor("layer_out", shape, F32, kind="ExternalOutput").ap())
    build_layer(nc, *args)
    result = run_bass_kernel_spmd(nc, [arrays], core_ids=[0])
    return result.results[0]["layer_out"]
```

```python
from contextlib import ExitStack

import numpy as np

import concourse.bass as bass
from concourse import mybir

F32 = mybir.dt.float32
BF16 = mybir.dt.bfloat16
I32 = mybir.dt.int32
ALU = mybir.AluOpType
ACT = mybir.ActivationFunctionType

P = 128
HEADS, HEAD_DIM = 16, 16
GROUP = 4
GROUPS = HEADS // GROUP
UNITS = 2 * GROUPS
SLOTS = 10
LEAD = 5
PARTS_Q = (0, 0, 1, 0, 2, 1)
PARTS_K = (0, 1, 0, 2, 0, 1)
TERMS = len(PARTS_Q)
SCORE_ROWS = TERMS * HEAD_DIM
MAX_PARTS = 3
MASKED = -1e30
LN_EPS = 1e-5
HUGE = 3e38
TWO_ONES = np.array([0x3F803F80], np.uint32).view(np.float32).item()
SWIGLU_ALPHA, LIMIT = 1.702, 7.0

KEY_BANKS = [[(h, 0, 0)] for h in range(4)] + [[(h, 3, 0), (h, 1, 128)] for h in range(4)] + [
    [(0, 2, 0), (1, 2, 256)], [(2, 2, 0), (3, 2, 256)]]
BANK_OF = {(h, kb): (n, col) for n, parts in enumerate(KEY_BANKS) for h, kb, col in parts}
MAX_BANKS = [[(h, 3, 0)] for h in range(4)] + [[(h, 2, 0), (h, 0, 384)] for h in range(4)] + [
    [(0, 1, 0), (1, 1, 256)], [(2, 1, 0), (3, 1, 256)]]
TRIANGLES = [(512, 2, 1), (512, 2, 1), (512, 2, 2), (512, 2, 2), (256, 4, 1)]


WEIGH_0 = 6
WEIGH_1, WEIGH_3, WEIGH_2 = 0, 1, 2
COPY_AFTER = 1
FINISH = 5
REST_AFTER, LOW_AFTER = 1, 5
NEG_LOW_AFTER = 2
PIECES = {(7, 8): ('k', 0),
          (0, 8): ('q', 0),
          (1, 8): ('k', 1),
          (2, 8): ('q', 1),
          (4, 8): ('k2', 0),
          (5, 8): ('k2', 1)}
TRANSPOSE_X = ((7, 2), (7, 5))
NEGATE_FIRST, NEGATE_SECOND = 7, 3
NEXT_BATCH = (5, 2)
LOAD_RESID, ADD_BIAS = (1, 0), (1, 5)
TRANSPOSE_Y = ((1, 2), (1, 5))
PROJECT_OUT = ((2, 3), (2, 4), (3, 3), (3, 4))
LAYER_NORMS = (3, 5)
APPLY_STEP = 2
FFN_SLOTS = (3, 4, 5, 7, 8, 9)
FFN_TAIL_STEP = 2


class Signal:

    def __init__(self, semaphore):
        self.semaphore, self.count = semaphore, 0


class Queue:

    def __init__(self):
        self.steps, self.waited = [], {}

    def add(self, make, waits=(), signal=None, by=1):
        fresh = []
        for point in waits:
            if point is None:
                continue
            sig, value = point
            if self.waited.get(id(sig), 0) < value:
                self.waited[id(sig)] = value
                fresh.append((sig.semaphore, value))
        self.steps.append((make, fresh, signal.semaphore if signal else None, by))
        if signal:
            signal.count += by
            return signal, signal.count
        return None

    def run(self, engine):
        for make, waits, semaphore, by in self.steps:
            for s, value in waits:
                engine.wait_ge(s, value)
            done = make(engine)
            if semaphore is not None:
                done.then_inc(semaphore, by)


def build_layer(nc, x, w_attn, b_attn, w_k2, b_k2, w_proj, b_proj,
                router_indices, routing_weights, w_up, b_up, w_down, b_down, out):
    batches, tokens, width = x.shape
    blocks = tokens // P
    halves = width // P
    heads_half = HEADS // halves
    experts, _, inter2 = w_up.shape
    inter = inter2 // 2
    routed = router_indices.shape[0]
    assert (tokens, width) == (512, 256) and routed == tokens and inter == width and batches > 1
    end_of_units = UNITS * batches
    n_rows = experts * inter2 // P

    ctx = ExitStack()
    with ctx:
        def sb(name, shape, dt=F32):
            return ctx.enter_context(nc.sbuf_tensor(name, shape, dt))

        def ps(name, cols):
            return ctx.enter_context(nc.psum_tensor(name, [P, cols], F32))

        def signal(name):
            return Signal(ctx.enter_context(nc.semaphore(name)))

        ident = sb("ident", [P, P])
        wq = sb("wq", [P, halves, 2 * halves, P])
        wk2 = sb("wk2", [P, halves, halves, P])
        wp = sb("wp", [P, halves, width])
        bias_qk = sb("bias_qk", [P, 3 * halves])
        bias2 = sb("bias2", [P, width])
        stack_q = [sb(f"stack_q{i}", [P, HEADS, tokens], BF16) for i in range(2)]
        stack_k = [sb(f"stack_k{i}", [P, HEADS, tokens], BF16) for i in range(2)]
        stack_k2 = [sb(f"stack_k2{i}", [P, HEADS, tokens], BF16) for i in range(2)]
        RING = 6
        KEY_DEPTH, MAX_DEPTH = 2, 3
        prob = [sb(f"prob{i}", [P, 1024]) for i in range(RING)]
        value1 = sb("value1", [P, blocks, HEADS, 32])
        value2 = sb("value2", [P, blocks, HEADS, 32])
        x_in = [sb(f"x_in{i}", [P, blocks, width]) for i in range(2)]
        x_next = sb("x_next", [P, blocks, width])
        resid = sb("resid", [P, blocks, width])
        y_sum = [sb(f"y_sum{i}", [P, blocks, width]) for i in range(2)]
        y_second = [sb(f"y_second{i}", [P, blocks, GROUP, HEAD_DIM]) for i in range(2)]
        y_t = sb("y_t", [P, halves, tokens])
        x_t = sb("x_t", [P, halves, tokens])
        heads_t = sb("heads_t", [P, tokens])
        part_h = [sb(f"part_h{i}", [P, tokens], BF16) for i in range(2)]
        part_m = [sb(f"part_m{i}", [P, tokens], BF16) for i in range(2)]
        part_l = [sb(f"part_l{i}", [P, tokens], BF16) for i in range(2)]
        part_r = [sb(f"part_r{i}", [P, tokens]) for i in range(2)]
        max_cols = [sb(f"max_cols{i}", [P, 2, HEADS, blocks]) for i in range(2)]
        neg_h = sb("neg_h", [64, P], BF16)
        neg_m = sb("neg_m", [64, P], BF16)
        neg_l = sb("neg_l", [64, P], BF16)
        neg_r = sb("neg_r", [64, P])
        mask_rows = [sb(f"mask_rows{i}", [P, tokens], BF16) for i in range(2)]
        mask_first = sb("mask_first", [P, P], BF16)
        JUNK = 2
        junk = [sb(f"junk{i}", [P, tokens], BF16) for i in range(JUNK)]
        den = sb("den", [P, blocks, GROUP])
        rden = sb("rden", [P, blocks, GROUP])
        stats = sb("stats", [P, blocks, 6])
        mean_var = sb("mean_var", [P, blocks, 2])
        var_eps = sb("var_eps", [P, blocks])
        log_var = sb("log_var", [P, blocks])
        rstd = sb("rstd", [P, 5, blocks])
        shift = sb("shift", [P, blocks])
        x1_routed = sb("x1_routed", [P, blocks, width])

        score_t = [ps(f"score_t{i}", 512) for i in range(KEY_DEPTH)]
        score = [ps(f"score{i}", 512) for i in range(MAX_DEPTH)]
        out_t = ps("out_t", 512)
        misc = ps("misc", 512)
        turn = ps("turn", 512)

        s_loadw = signal("s_loadw")
        s_rows = signal("s_rows")
        s_const = signal("s_const")
        s_consta = signal("s_consta")
        s_x = [signal(f"s_x{i}") for i in range(2)]
        s_next = signal("s_next")
        s_resid_in = signal("s_resid_in")
        s_stack = {(kind, hf): signal(f"s_stack_{kind}{hf}") for kind in ("q", "k", "k2") for hf in range(halves)}
        s_maxrow = [signal(f"s_maxrow{i}") for i in range(2)]
        s_out = signal("s_out")
        s_score_t = signal("s_score_t")
        s_score = signal("s_score")
        s_pv = signal("s_pv")
        s_pe = signal("s_pe")
        s_exp = signal("s_exp")
        s_act = signal("s_act")
        s_max = signal("s_max")
        s_dve = signal("s_dve")
        s_mask = signal("s_mask")
        s_pool = signal("s_pool")
        s_ffn_up = [signal(f"s_ffn_up{i}") for i in range(2)]
        s_ffn_down = [signal(f"s_ffn_down{i}") for i in range(2)]
        s_ffn_in = signal("s_ffn_in")

        pe, act, dve, pool, sp = (Queue() for _ in range(5))

        raw_attn = prob[0][:, :].rearrange("p (h n) -> p h n", h=halves)
        raw_k2 = prob[1][:, 0:halves * width].rearrange("p (h n) -> p h n", h=halves)
        raw_bias = prob[2][:, 0:width]
        sp.add(lambda e: e.dma_start(raw_attn, w_attn.rearrange("(h p) n -> p h n", p=P)), signal=s_loadw, by=16)
        sp.add(lambda e: e.dma_start(raw_k2, w_k2.rearrange("(h p) n -> p h n", p=P)), signal=s_loadw, by=16)
        sp.add(lambda e: e.dma_start(wp[:, :, :], w_proj.rearrange("(h p) n -> p h n", p=P)), signal=s_loadw, by=16)
        sp.add(lambda e: e.dma_start(raw_bias, b_proj.rearrange("(o n) -> o n", o=1).to_broadcast([P, width])),
               signal=s_loadw, by=16)
        bias_rows = prob[3][0:3 * halves, 0:P]
        bias_sorted = prob[3][0:3 * halves, P:2 * P]
        sp.add(lambda e: e.dma_start(prob[3][0:2 * halves, 0:P], b_attn.rearrange("(r p) -> r p", p=P)), signal=s_loadw, by=16)
        sp.add(lambda e: e.dma_start(prob[3][2 * halves:3 * halves, 0:P], b_k2.rearrange("(r p) -> r p", p=P)), signal=s_loadw, by=16)
        weights_loaded = (s_loadw, s_loadw.count)

        pool.add(lambda e: e.memset(ident[:, :], 1.0), signal=s_const)
        made = pool.add(lambda e: e.memset(x_next[:, :, :], 0.0), signal=s_const)
        next_zeroed = made
        pool.add(lambda e: e.memset(value1[:, :, :, :], 1.0), signal=s_const)
        pool.add(lambda e: e.memset(value2[:, :, :, :], 1.0), signal=s_const)
        for tile in (mask_rows[0], mask_rows[1], mask_first):
            pool.add(lambda e, tile=tile: e.memset(tile[:, :], 0.0), signal=s_const)
        made = (s_const, s_const.count)
        pool.add(lambda e: e.affine_select(out=ident[:, :], in_=ident[:, :], compare_op=ALU.is_equal, fill=0.0,
                                           base=0, pattern=[[1, P]], channel_multiplier=-1),
                 waits=[made], signal=s_const)
        for a in range(2):
            tri = mask_rows[a][:, tokens - P:tokens]
            pool.add(lambda e, tri=tri, a=a: e.affine_select(
                out=tri, in_=tri, compare_op=ALU.is_ge, fill=MASKED, base=-a, pattern=[[-1, P]],
                channel_multiplier=1), signal=s_const)
        made = pool.add(lambda e: e.affine_select(
            out=mask_first[:, :], in_=mask_first[:, :], compare_op=ALU.is_ge, fill=MASKED, base=-1,
            pattern=[[-1, P]], channel_multiplier=1), signal=s_const)
        constants = made

        R = SCORE_ROWS

        def as_words(stack, rows):
            return stack[R:R + rows, :, :].rearrange("p h t -> p (h t)").bitcast(F32)

        made = dve.add(lambda e: e.memset(as_words(stack_k2[0], 2 * MAX_PARTS), TWO_ONES), signal=s_consta)
        sp.add(lambda e: e.dma_start(stack_k[0][R:R + MAX_PARTS, :, :], stack_k2[0][R + MAX_PARTS:R + 2 * MAX_PARTS, :, :]),
               waits=[made], signal=s_rows, by=16)
        sp.add(lambda e: e.dma_start(stack_k[1][R:R + MAX_PARTS, :, :], stack_k2[0][R + MAX_PARTS:R + 2 * MAX_PARTS, :, :]),
               signal=s_rows, by=16)
        sp.add(lambda e: e.dma_start(stack_k2[1][R + MAX_PARTS:R + 2 * MAX_PARTS, :, :], stack_k2[0][R + MAX_PARTS:R + 2 * MAX_PARTS, :, :]),
               signal=s_rows, by=16)
        made = dve.add(lambda e: e.memset(as_words(stack_k2[0], MAX_PARTS), 0.0), waits=[made], signal=s_consta)
        rows_ready = sp.add(lambda e: e.dma_start(stack_k2[1][R:R + MAX_PARTS, :, :], stack_k2[0][R:R + MAX_PARTS, :, :]),
                            waits=[made], signal=s_rows, by=16)
        dve.add(lambda e: e.memset(mask_first[0:1, 0:1], 0.0), waits=[constants], signal=s_consta)
        for piece in range(2 * halves):
            made = dve.add(lambda e, piece=piece: e.tensor_copy(
                wq[:, :, piece, :].rearrange("p c (d h) -> p c d h", d=HEAD_DIM),
                raw_attn[:, :, piece * P:(piece + 1) * P].rearrange("p c (h d) -> p c d h", d=HEAD_DIM)),
                waits=[weights_loaded], signal=s_consta)
        for hf in range(halves):
            made = dve.add(lambda e, hf=hf: e.tensor_copy(
                wk2[:, :, hf, :].rearrange("p c (d h) -> p c d h", d=HEAD_DIM),
                raw_k2[:, :, hf * P:(hf + 1) * P].rearrange("p c (h d) -> p c d h", d=HEAD_DIM)),
                signal=s_consta)
        dve.add(lambda e: e.tensor_tensor(bias2[:, :], raw_bias, raw_bias, ALU.add), signal=s_consta)
        made = dve.add(lambda e: e.tensor_copy(bias_sorted.rearrange("r (d h) -> r d h", d=HEAD_DIM),
                                               bias_rows.rearrange("r (h d) -> r d h", d=HEAD_DIM)), signal=s_consta)
        made = pe.add(lambda e: e.transpose(misc[:, 0:3 * halves], bias_sorted, ident[0:3 * halves, 0:3 * halves]),
                      waits=[made, constants], signal=s_pe)
        weights_ready = dve.add(lambda e: e.tensor_copy(bias_qk[:, :], misc[:, 0:3 * halves]), waits=[made], signal=s_consta)

        x_loaded, next_loaded, resid_loaded = {}, {}, {}
        x_t_ready = {}
        x_t_read = {}
        stack_ready = {}
        unit_scores_done = {}
        unit_max_done = {}
        unit_max_scores = {}
        max_rows_ready = {}
        exp_done, mask_done = {}, {}
        pair_read = {}
        bank_max = {}
        unit_pv_done = {}
        heads_copied = {}
        value1_ready, value2_ready = {}, {}
        y_added = {}
        state = {"misc_read": [weights_ready, constants], "turn_read": [constants], "junk": [None] * JUNK, "piece": 0, "heads_read": None,
                 "max_copied": None, "neg_sent": None, "den": None, "y_t_read": None,
                 "resid_free": None, "value1_free": None, "x_free": {}, "next_free": next_zeroed,
                 "neg_r": None}
        piece_history = []

        later = {}

        def put_off(slots, steps):
            later.setdefault(state["now"] + slots, []).append(steps)

        def run_put_off(now):
            for steps in later.pop(now, []):
                steps()

        def unit_parts(unit):
            return unit // UNITS, unit % UNITS // GROUPS, unit % GROUPS

        def load_x(b):
            x_loaded[b] = sp.add(lambda e: e.dma_start(x_in[b % 2][:, :, :], x[b].rearrange("(t p) c -> p t c", p=P)),
                                 waits=[state["x_free"].get(b)], signal=s_x[b % 2], by=16)

        def load_next(b):
            last = blocks - 1
            sp.add(lambda e: e.dma_start(x_next[:, 0:last, :], x[b, 1:1 + last * P, :].rearrange("(t p) c -> p t c", p=P)),
                   waits=[state["next_free"]], signal=s_next, by=16)
            next_loaded[b] = sp.add(lambda e: e.dma_start(x_next[0:P - 1, last, :], x[b, 1 + last * P:tokens, :]),
                                    signal=s_next, by=16)

        def load_resid(b):
            resid_loaded[b] = sp.add(lambda e: e.dma_start(resid[:, :, :], x[b].rearrange("(t p) c -> p t c", p=P)),
                                     waits=[state["resid_free"]], signal=s_resid_in, by=16)

        def transpose_x(b, hf):
            src = x_in[b % 2]
            for t in range(blocks):
                done = pe.add(lambda e, t=t: e.transpose(misc[:, t * P:(t + 1) * P], src[:, t, hf * P:(hf + 1) * P], ident[:, :]),
                              waits=[x_loaded[b]] + state["misc_read"], signal=s_pe if t == blocks - 1 else None)
            state["misc_read"] = []

            def copy_step():
                x_t_ready[b] = act.add(lambda e: e.activation(x_t[:, hf, :], misc[:, :], ACT.Copy),
                                       waits=[done, x_t_read.get(b - 1)], signal=s_act)
                state["misc_read"] = [x_t_ready[b]]

            put_off(1, copy_step)

        def project_piece(kind, b, hf, c):
            n = state["piece"]
            i = n % 2
            old = piece_history[n - 2] if n >= 2 else {}
            piece = {"q": hf, "k": halves + hf, "k2": 2 * halves + hf}[kind]
            w = wk2[:, c, hf, :] if kind == "k2" else wq[:, c, piece, :]
            done = pe.add(lambda e: e.matmul(misc[:, :], w, x_t[:, c, :], start=(c == 0), stop=(c == halves - 1)),
                          waits=[x_t_ready[b], weights_ready] + state["misc_read"],
                          signal=s_pe if c == halves - 1 else None)
            if c < halves - 1:
                return
            state["piece"] += 1
            x_t_read[b] = done
            bias = bias_qk[:, piece:piece + 1]
            high = act.add(lambda e: e.activation(part_h[i][:, :], misc[:, :], ACT.Identity, bias=bias),
                           waits=[done, weights_ready, old.get("sent")], signal=s_act)
            record = {"parts": (part_h[i], part_m[i], part_l[i])}
            piece_history.append(record)
            state["misc_read"] = []

            def rest_step():
                record["rest"] = dve.add(lambda e: e.scalar_tensor_tensor(
                    out=part_r[i][:, :], in0=misc[:, :], scalar=bias, in1=part_h[i][:, :], op0=ALU.add,
                    op1=ALU.subtract), waits=[high, old.get("low")], signal=s_dve)
                state["misc_read"] = [record["rest"]]

            def low_steps():
                middle = act.add(lambda e: e.activation(part_m[i][:, :], part_r[i][:, :], ACT.Copy),
                                 waits=[record["rest"], old.get("sent")], signal=s_act)
                record["low"] = pool.add(lambda e: e.tensor_tensor(part_l[i][:, :], part_r[i][:, :], part_m[i][:, :], ALU.subtract),
                                         waits=[middle, old.get("sent")], signal=s_pool)

            put_off(REST_AFTER, rest_step)
            put_off(LOW_AFTER, low_steps)
            put_off(LOW_AFTER + 1, lambda: send_piece(kind, b, hf, record))

        def send_piece(kind, b, hf, record):
            stack = {"q": stack_q, "k": stack_k, "k2": stack_k2}[kind][b % 2]
            last_group = (hf + 1) * GROUPS // halves - 1
            reader = UNITS * (b - 2) + (0 if kind == "k" else GROUPS) + last_group
            free = unit_scores_done.get(reader)
            for term, part in enumerate(PARTS_Q if kind == "q" else PARTS_K):
                sent = sp.add(lambda e, term=term, part=part: e.dma_start(
                    stack[term * HEAD_DIM:(term + 1) * HEAD_DIM, hf * heads_half:(hf + 1) * heads_half, :],
                    record["parts"][part][:, :]), waits=[record["low"], free, constants], signal=s_stack[kind, hf], by=16)
            stack_ready[kind, b, hf] = record["sent"] = sent

        def stacks(unit):
            b, a, g = unit_parts(unit)
            kind = "k2" if a else "k"
            keys = (stack_k2 if a else stack_k)[b % 2]
            hf = g * halves // GROUPS
            return stack_q[b % 2], keys, [stack_ready["q", b, hf], stack_ready[kind, b, hf]]

        def max_bank(unit, n):
            b, a, g = unit_parts(unit)
            queries, keys, ready = stacks(unit)
            number = len(MAX_BANKS) * unit + n
            bank = score[number % MAX_DEPTH]
            for h, qb, col in MAX_BANKS[n]:
                head, keys_n = GROUP * g + h, P * (qb + 1)
                last = (h, qb, col) == MAX_BANKS[n][-1]
                done = pe.add(lambda e, head=head, qb=qb, col=col, keys_n=keys_n: e.matmul(
                    bank[:, col:col + keys_n], queries[0:SCORE_ROWS, head, qb * P:(qb + 1) * P],
                    keys[0:SCORE_ROWS, head, 0:keys_n], start=True, stop=True),
                    waits=ready + [bank_max.get(number - MAX_DEPTH)], signal=s_score if last else None)
            unit_max_scores[unit] = done
            for h, qb, col in MAX_BANKS[n]:
                head, keys_n = GROUP * g + h, P * (qb + 1)
                mask = mask_first[:, :] if a and qb == 0 else mask_rows[a][:, tokens - keys_n:tokens]
                k = s_max.count % JUNK
                target = max_cols[b % 2]
                state["junk"][k] = bank_max[number] = dve.add(
                    lambda e, head=head, qb=qb, col=col, keys_n=keys_n, mask=mask, k=k: e.tensor_tensor_reduce(
                        junk[k][:, 0:keys_n], bank[:, col:col + keys_n], mask, 1.0, -3e38, ALU.add, ALU.max,
                        target[:, a, head, qb:qb + 1]),
                    waits=[done, constants, state["junk"][k]], signal=s_max)
            unit_max_done[unit] = bank_max[number]

        def negate_maxima(b, a):
            src = max_cols[b % 2][:, a, :, :].rearrange("p h q -> p (h q)")
            n = HEADS * blocks
            done = pe.add(lambda e: e.transpose(turn[0:n, 0:P], src, ident[:, :]),
                          waits=[unit_max_done[UNITS * b + GROUPS * a + GROUPS - 1]] + state["turn_read"], signal=s_pe)
            high = act.add(lambda e: e.activation(neg_h[:, :], turn[0:n, 0:P], ACT.Copy, scale=-1.0),
                           waits=[done, state["neg_sent"]], signal=s_act)
            state["turn_read"] = []
            made = {}

            def rest_step():
                made["rest"] = dve.add(lambda e: e.scalar_tensor_tensor(
                    out=neg_r[:, :], in0=turn[0:n, 0:P], scalar=-1.0, in1=neg_h[:, :], op0=ALU.mult,
                    op1=ALU.subtract), waits=[high, state["neg_r"]], signal=s_dve)
                state["turn_read"] = [made["rest"]]

            def low_steps():
                middle = act.add(lambda e: e.activation(neg_m[:, :], neg_r[:, :], ACT.Copy),
                                 waits=[made["rest"], state["neg_sent"]], signal=s_act)
                low = pool.add(lambda e: e.tensor_tensor(neg_l[:, :], neg_r[:, :], neg_m[:, :], ALU.subtract),
                               waits=[middle, state["neg_sent"]], signal=s_pool)
                state["neg_r"] = low
                free = unit_scores_done.get(UNITS * (b - 2) + UNITS - 1)
                for part, tile in enumerate((neg_h, neg_m, neg_l)):
                    row = SCORE_ROWS + MAX_PARTS * a + part
                    sent = sp.add(lambda e, row=row, tile=tile: e.dma_start(stack_q[b % 2][row:row + 1, :, :], tile[:, :]),
                                  waits=[low, free], signal=s_maxrow[a], by=16)
                max_rows_ready[b, a] = state["neg_sent"] = sent

            put_off(1, rest_step)
            put_off(NEG_LOW_AFTER, low_steps)

        def key_bank(unit, n):
            b, a, g = unit_parts(unit)
            queries, keys, ready = stacks(unit)
            number = SLOTS * unit + n
            pair = number // 2
            bank = score_t[number % KEY_DEPTH]
            rows = SCORE_ROWS + MAX_PARTS * (a + 1)
            ready = ready + [max_rows_ready[b, 0], max_rows_ready[b, a], rows_ready]
            for h, kb, col in KEY_BANKS[n]:
                head, queries_n = GROUP * g + h, tokens - P * kb
                last = (h, kb, col) == KEY_BANKS[n][-1]
                done = pe.add(lambda e, head=head, kb=kb, col=col, queries_n=queries_n: e.matmul(
                    bank[:, col:col + queries_n], keys[0:rows, head, kb * P:(kb + 1) * P],
                    queries[0:rows, head, kb * P:tokens], start=True, stop=True),
                    waits=ready + [exp_done.get(number - KEY_DEPTH)], signal=s_score_t if last else None)
            unit_scores_done[unit] = done
            tile = prob[pair % RING]
            exp_done[number] = act.add(
                lambda e: e.activation(tile[:, n % 2 * 512:n % 2 * 512 + 512], bank[:, :], ACT.Exp,
                                       scale=1.0 / np.sqrt(HEAD_DIM).item()),
                waits=[done, pair_read.get(pair - RING), weights_ready], signal=s_exp)
            if n % 2 == 0:
                return
            step, runs, cut = TRIANGLES[n // 2]
            view = tile[:, :].rearrange("p (r s) -> p r s", s=step)[:, :, 0:cut * P]
            pattern = [[0, runs], [0, cut], [1, P]]
            mask_done[pair] = pool.add(lambda e: e.affine_select(
                out=view, in_=view, compare_op=ALU.is_ge, fill=0.0, base=-a, pattern=pattern,
                channel_multiplier=-1), waits=[exp_done[number]], signal=s_mask)

        def weigh(unit, kb, first, count, start=False, stop=False):
            b, a, g = unit_parts(unit)
            value = value2 if a else value1
            ready = value2_ready[b, g] if a else value1_ready[b]
            for h in range(GROUP):
                n, col = BANK_OF[h, kb]
                pair = (SLOTS * unit + n) // 2
                at = n % 2 * 512 + col + first - P * kb
                done = pe.add(lambda e, h=h, pair=pair, at=at: e.matmul(
                    out_t[32 * h:32 * h + 32, first:first + count], value[:, kb, GROUP * g + h, :],
                    prob[pair % RING][:, at:at + count], start=start, stop=stop, skip_group_check=True),
                    waits=[mask_done[pair], ready, heads_copied.get(unit - 1)],
                    signal=s_pv if h == GROUP - 1 else None)
            return done

        def weigh_slot(slot, unit):
            pair = SLOTS // 2 * unit
            if 0 <= unit < end_of_units:
                if slot == WEIGH_0:
                    pair_read[pair] = pair_read[pair + 1] = weigh(unit, 0, 0, tokens, start=True)
            before = unit - 1
            if not 0 <= before < end_of_units:
                return
            pair = SLOTS // 2 * before
            if slot == WEIGH_1:
                weigh(before, 1, P, 3 * P)
            if slot == WEIGH_3:
                pair_read[pair + 2] = pair_read[pair + 3] = weigh(before, 3, 3 * P, P)
            if slot == WEIGH_2:
                pair_read[pair + 4] = unit_pv_done[before] = weigh(before, 2, 2 * P, 2 * P, stop=True)
                put_off(COPY_AFTER, lambda: copy_heads(before))

        def copy_heads(unit):
            heads_copied[unit] = act.add(lambda e: e.activation(heads_t[:, :], out_t[:, :], ACT.Copy),
                                         waits=[unit_pv_done[unit], state["heads_read"]], signal=s_act)

        def finish_unit(unit):
            b, a, g = unit_parts(unit)
            for t in range(blocks):
                done = pe.add(lambda e, t=t: e.transpose(turn[:, t * P:(t + 1) * P], heads_t[:, t * P:(t + 1) * P], ident[:, :]),
                              waits=[heads_copied[unit]] + state["turn_read"], signal=s_pe if t == blocks - 1 else None)
            state["heads_read"] = done
            heads = turn[:, :].rearrange("p (t h w) -> p t h w", t=blocks, h=GROUP)
            chans = slice(g * GROUP * HEAD_DIM, (g + 1) * GROUP * HEAD_DIM)
            y = y_sum[b % 2][:, :, chans].rearrange("p t (h d) -> p t h d", d=HEAD_DIM)
            second = y_second[g % 2][:, :, :, :]
            made = {}

            def normalise():
                sums, ready = heads[:, :, :, HEAD_DIM], done
                if a:
                    ready = dve.add(lambda e: e.tensor_scalar(den[:, :, :], sums, 1e-30, None, ALU.max),
                                    waits=[done, state["den"]], signal=s_dve)
                inverse = dve.add(lambda e: e.reciprocal(rden[:, :, :], den[:, :, :] if a else sums),
                                  waits=[ready, state["den"]], signal=s_dve)
                wide = bass.AP(rden[:, :, :].tensor, rden[:, :, :].offset,
                               [list(rden[:, :, :].ap[0]), [GROUP, blocks], [1, GROUP], [0, HEAD_DIM]])
                made["normal"] = dve.add(
                    lambda e: e.tensor_tensor(second if a else y, heads[:, :, :, 0:HEAD_DIM], wide, ALU.mult),
                    waits=[inverse, state.get(("second", g % 2)) if a else state.get(("y_t", b - 2))], signal=s_dve)
                state["den"] = made["normal"]
                state["turn_read"] = [made["normal"]]

            def add_up():
                if a:
                    y_added[b] = state["second", g % 2] = pool.add(
                        lambda e: e.tensor_tensor(y, y, second, ALU.add),
                        waits=[made["normal"], value2_ready[b, g]], signal=s_pool)
                    return
                nxt = x_next[:, :, chans].rearrange("p t (h d) -> p t h d", d=HEAD_DIM)
                value2_ready[b, g] = state["next_free"] = pool.add(lambda e: e.tensor_tensor(
                    value2[:, :, GROUP * g:GROUP * g + GROUP, 0:HEAD_DIM], nxt, y, ALU.subtract),
                    waits=[made["normal"], next_loaded[b], constants, unit_pv_done.get(UNITS * (b - 1) + GROUPS + g)],
                    signal=s_pool)

            state["turn_read"] = []
            put_off(1, normalise)
            put_off(5, add_up)

        def transpose_y(b, hf):
            src = y_sum[b % 2]
            for t in range(blocks):
                done = pe.add(lambda e, t=t: e.transpose(misc[:, t * P:(t + 1) * P], src[:, t, hf * P:(hf + 1) * P], ident[:, :]),
                              waits=[y_added[b]] + state["misc_read"], signal=s_pe if t == blocks - 1 else None)
            state["y_t", b] = done
            state["misc_read"] = []

            def copy_step():
                state["y_t_ready"] = act.add(lambda e: e.activation(y_t[:, hf, :], misc[:, :], ACT.Copy),
                                             waits=[done, state["y_t_read"]], signal=s_act)
                state["misc_read"] = [state["y_t_ready"]]

            put_off(1, copy_step)

        def project_out(b, pair, j):
            t = 2 * pair + j
            for c in range(halves):
                done = pe.add(lambda e, c=c: e.matmul(
                    misc[:, j * width:(j + 1) * width], y_t[:, c, t * P:(t + 1) * P], wp[:, c, :],
                    start=(c == 0), stop=(c == halves - 1)),
                    waits=[state["y_t_ready"], weights_loaded] + state["misc_read"],
                    signal=s_pe if (j, c) == (1, halves - 1) else None)
            if j == 0:
                return
            state["y_t_read"] = done
            rows = resid[:, 2 * pair:2 * pair + 2, :]
            state["misc_read"] = []

            def add_step():
                state["attended"] = dve.add(lambda e: e.tensor_tensor(
                    rows, misc[:, :].rearrange("p (t c) -> p t c", t=2), rows, ALU.add),
                    waits=[done, state["biased"]], signal=s_dve)
                state["misc_read"] = [state["attended"]]

            put_off(1, add_step)

        def add_bias(b):
            wide = bass.AP(bias2[:, :].tensor, bias2[:, :].offset, [list(bias2[:, :].ap[0]), [0, blocks], [1, width]])
            state["biased"] = pool.add(lambda e: e.tensor_tensor(resid[:, :, :], resid[:, :, :], wide, ALU.add),
                                       waits=[resid_loaded[b], weights_ready], signal=s_pool)

        def variance_eps(aggregated):
            return pool.add(lambda e: e.tensor_scalar(var_eps[:, :], mean_var[:, :, 1], LN_EPS, None, ALU.add),
                            waits=[aggregated], signal=s_pool)

        def guess_rstd(v):
            log = act.add(lambda e: e.activation(log_var[:, :], var_eps[:, :], ACT.Ln), waits=[v], signal=s_act)
            return act.add(lambda e: e.activation(rstd[:, 0, :], log_var[:, :], ACT.Exp, scale=-0.5),
                           waits=[log, state.get("shifted")], signal=s_act)

        def refine_rstd(guess):
            s = pool.add(lambda e: e.tensor_tensor(rstd[:, 1, :], rstd[:, 0, :], rstd[:, 0, :], ALU.mult),
                         waits=[guess], signal=s_pool)
            s = pool.add(lambda e: e.tensor_tensor(rstd[:, 2, :], rstd[:, 1, :], var_eps[:, :], ALU.mult),
                         waits=[s], signal=s_pool)
            s = pool.add(lambda e: e.tensor_scalar(rstd[:, 3, :], rstd[:, 2, :], -0.5, 1.5, ALU.mult, ALU.add),
                         waits=[s], signal=s_pool)
            s = pool.add(lambda e: e.tensor_tensor(rstd[:, 4, :], rstd[:, 3, :], rstd[:, 0, :], ALU.mult),
                         waits=[s, state.get("applied")], signal=s_pool)
            s = pool.add(lambda e: e.tensor_tensor(log_var[:, :], mean_var[:, :, 0], rstd[:, 4, :], ALU.mult),
                         waits=[s], signal=s_pool)
            s = pool.add(lambda e: e.tensor_scalar(shift[:, :], log_var[:, :], -1.0, None, ALU.mult),
                         waits=[s], signal=s_pool)
            state["shifted"] = s
            return s

        def apply_block(dst, src, t, ready):
            state["applied"] = act.add(lambda e: e.activation(dst[:, t, :], src[:, t, :], ACT.Identity,
                                                              bias=shift[:, t:t + 1], scale=rstd[:, 4, t:t + 1]),
                                       waits=[ready], signal=s_act)
            return state["applied"]

        def layer_norm(dst, src, ready, after):
            made = {}

            def stats_step(t):
                made["s", t] = dve.add(lambda e: e.bn_stats(stats[:, t, :], src[:, t, :]),
                                       waits=[ready(), state.get("aggregated")], signal=s_dve)

            def aggregate():
                for t in range(blocks):
                    done = dve.add(lambda e, t=t: e.bn_aggr(mean_var[:, t, :], stats[:, t, :]),
                                   waits=[made["s", blocks - 1], state.get("shifted")], signal=s_dve)
                state["aggregated"] = done

            for t in range(blocks):
                put_off(1 + t, lambda t=t: stats_step(t))
            put_off(1 + blocks, aggregate)
            put_off(5 + blocks, lambda: made.update(v=variance_eps(state["aggregated"])))
            put_off(6 + blocks, lambda: made.update(g=guess_rstd(made["v"])))
            put_off(7 + blocks, lambda: made.update(r=refine_rstd(made["g"])))

            def apply_step(t):
                made["a"] = apply_block(dst, src, t, made["r"])

            for t in range(blocks):
                put_off(9 + blocks + APPLY_STEP * t, lambda t=t: apply_step(t))
            put_off(9 + blocks + APPLY_STEP * (blocks - 1) + 1, lambda: after(made["a"]))

        def store(b, ready):
            state["resid_free"] = sp.add(lambda e: e.dma_start(out[b].rearrange("(t p) c -> p t c", p=P), resid[:, :, :]),
                                         waits=[ready], signal=s_out, by=16)

        def extra(unit, slot):
            place = unit % UNITS
            ahead = (unit - place) // UNITS
            for c in range(halves):
                b = ahead + (2 if place == UNITS - 1 else 1)
                if (place, slot - c) in PIECES and 0 <= b < batches:
                    kind, hf = PIECES[place, slot - c]
                    project_piece(kind, b, hf, c)
            if (place, slot) in TRANSPOSE_X and 0 <= ahead + 2 < batches:
                transpose_x(ahead + 2, TRANSPOSE_X.index((place, slot)))
            if slot == 0 and place == NEGATE_FIRST and 0 <= ahead + 1 < batches:
                negate_maxima(ahead + 1, 0)
            if slot == 0 and place == NEGATE_SECOND and 0 <= ahead < batches:
                negate_maxima(ahead, 1)
            if (place, slot) == NEXT_BATCH and 0 <= ahead + 1 < batches:
                b = ahead + 1
                value1_ready[b] = dve.add(lambda e: e.tensor_copy(
                    value1[:, :, :, 0:HEAD_DIM], x_in[b % 2][:, :, :].rearrange("p t (h d) -> p t h d", d=HEAD_DIM)),
                    waits=[x_loaded[b], constants, unit_pv_done.get(UNITS * (b - 1) + GROUPS - 1)], signal=s_dve)
                state["x_free"][b + 2] = value1_ready[b]
                load_next(b)
                if b + 2 < batches:
                    load_x(b + 2)
            b = ahead - 1
            if not 0 <= b < batches:
                return
            if (place, slot) == LOAD_RESID:
                load_resid(b)
            if (place, slot) == ADD_BIAS:
                add_bias(b)
            if (place, slot) in TRANSPOSE_Y:
                transpose_y(b, TRANSPOSE_Y.index((place, slot)))
            if (place, slot) in PROJECT_OUT:
                k = PROJECT_OUT.index((place, slot))
                project_out(b, k // 2, k % 2)
            if (place, slot) == LAYER_NORMS:
                if b == 0:
                    def keep(done):
                        state["resid_free"] = state["x1_routed"] = done
                    layer_norm(x1_routed, resid, lambda: state["attended"], keep)
                else:
                    layer_norm(resid, resid, lambda: state["attended"], lambda done: layer_norm(
                        resid, resid, lambda: done, lambda done: store(b, done)))

        spare = batches % 2
        last_batch = UNITS * (batches - 1)
        ffn_first = last_batch + UNITS - LEAD
        banks = [score[i][:, :] for i in range(MAX_DEPTH)]
        GATE, UP, DOWN = range(3)

        def in_stack(stack, first, shape):
            n = int(np.prod(shape))
            flat = stack[spare][:, :, :].rearrange("p h t -> p (h t)")[:, 2 * first:2 * (first + n)].bitcast(F32)
            names = "abcd"[:len(shape)]
            sizes = dict(zip(names, shape))
            return flat.rearrange(f"p ({' '.join(names)}) -> p {' '.join(names)}", **sizes)

        weight_cols = halves * (inter2 + width)
        up_w = [in_stack(stack_k, i * weight_cols, (halves, inter2)) for i in range(2)]
        down_w = [in_stack(stack_k, i * weight_cols + halves * inter2, (halves, width)) for i in range(2)]
        x1_t = in_stack(stack_k, 2 * weight_cols, (halves, tokens))
        gate = [in_stack(stack_q, (0 + i) * tokens, (tokens,)) for i in range(2)]
        sigm = [in_stack(stack_q, (2 + i) * tokens, (tokens,)) for i in range(2)]
        lift = [in_stack(stack_q, (4 + i) * tokens, (tokens,)) for i in range(2)]
        ffn = in_stack(stack_q, 6 * tokens, (blocks, width))
        inner = [in_stack(stack_k2, 2048 + halves * tokens * i, (halves, tokens)) for i in range(2)]
        down_b = in_stack(stack_k2, 0, (width,))
        up_b = in_stack(stack_k2, 256, (experts * inter2 // P,))
        chosen = in_stack(stack_k2, 512, (blocks, 2))
        same = in_stack(stack_k2, 528, (blocks, 2))
        route = in_stack(stack_k2, 544, (blocks, experts))
        coef = in_stack(stack_k2, 576, (blocks, experts))
        coef_t = in_stack(stack_k2, 1024, (tokens,))
        up_b_rows = in_stack(stack_k2, 1536, (P,))
        chosen_i = in_stack(stack_k2, 1664, (blocks, 2)).bitcast(I32)
        up_b_odd = in_stack(stack_k2, 1792, (n_rows,))
        gates_rows = up_b_rows[0:n_rows, :].rearrange("r (c two) -> r two c", two=2)
        f = {"bank": [None] * MAX_DEPTH}

        def load_up(ex, reader):
            f["up_w", ex] = sp.add(lambda e: e.dma_start(up_w[ex % 2], w_up[ex].rearrange("(h p) n -> p h n", p=P)),
                                   waits=[reader], signal=s_ffn_up[ex % 2], by=16)

        def load_down(ex, reader):
            f["down_w", ex] = sp.add(lambda e: e.dma_start(down_w[ex % 2], w_down[ex].rearrange("(h p) n -> p h n", p=P)),
                                     waits=[reader], signal=s_ffn_down[ex % 2], by=16)

        def ffn_loads():
            f["free"] = free = unit_scores_done[last_batch - 1]
            f["bank"] = [unit_max_done[end_of_units - 1]] * MAX_DEPTH
            sp.add(lambda e: e.dma_start(chosen_i, router_indices.rearrange("(t p) k -> p t k", p=P)),
                   waits=[free], signal=s_ffn_in, by=16)
            sp.add(lambda e: e.dma_start(route, routing_weights.rearrange("(t p) k -> p t k", p=P)), signal=s_ffn_in, by=16)
            sp.add(lambda e: e.dma_start(down_b[0:experts, :], b_down), signal=s_ffn_in, by=16)
            f["loaded"] = sp.add(lambda e: e.dma_start(up_b_rows[0:n_rows, :], b_up.rearrange("x (r p) -> (x r) p", p=P)),
                                 signal=s_ffn_in, by=16)
            for ex in range(2):
                load_up(ex, None)
                load_down(ex, None)
            put_off(2, coefficients)

        def coefficients():
            step = dve.add(lambda e: e.tensor_copy(chosen, chosen_i), waits=[f["loaded"], f["free"]], signal=s_dve)
            for ex in range(experts):
                step = dve.add(lambda e, ex=ex: e.tensor_scalar(same, chosen, float(ex), None, ALU.is_equal),
                               waits=[step], signal=s_dve)
                step = dve.add(lambda e, ex=ex: e.tensor_tensor(coef[:, :, ex], same[:, :, 0], same[:, :, 1], ALU.add),
                               waits=[step], signal=s_dve)
            f["coef"] = dve.add(lambda e: e.tensor_tensor(coef, coef, route, ALU.mult), waits=[step], signal=s_dve)

        def transpose_x1(hf, k):
            for t in range(blocks):
                done = pe.add(lambda e, t=t: e.transpose(banks[k][:, t * P:(t + 1) * P], x1_routed[:, t, hf * P:(hf + 1) * P], ident[:, :]),
                              waits=[state["x1_routed"], f["bank"][k]], signal=s_pe if t == blocks - 1 else None)

            def copy_step():
                f["x1_t"] = f["bank"][k] = act.add(lambda e: e.activation(x1_t[:, hf, :], banks[k], ACT.Copy),
                                                   waits=[done, f["free"]], signal=s_act)
            put_off(1, copy_step)

        def transpose_up_bias(k):
            for two in range(2):
                done = pe.add(lambda e, two=two: e.transpose(banks[k][0:64, two * n_rows:(two + 1) * n_rows],
                                                             gates_rows[:, two, :], ident[0:n_rows, 0:n_rows]),
                              waits=[f["loaded"], f["bank"][k]], signal=s_pe if two else None)
            turned = banks[k][0:64, 0:2 * n_rows].rearrange("p (w x f two) -> p w x f two", w=2, x=experts, two=2)

            def copy_step():
                even = act.add(lambda e: e.activation(up_b[0:64, :].rearrange("p (w x f) -> p w x f", w=2, x=experts),
                                                      turned[:, :, :, :, 0], ACT.Copy), waits=[done, f["free"]], signal=s_act)
                odd = act.add(lambda e: e.activation(up_b_odd[0:64, :].rearrange("p (w x f) -> p w x f", w=2, x=experts),
                                                     turned[:, :, :, :, 1], ACT.Copy), waits=[done], signal=s_act)
                f["bank"][k] = odd
                f["up_b"] = sp.add(lambda e: e.dma_start(up_b[64:128, :], up_b_odd[0:64, :]), waits=[odd, even],
                                   signal=s_ffn_in, by=16)
            put_off(1, copy_step)

        def transpose_coef(k):
            for t in range(blocks):
                done = pe.add(lambda e, t=t: e.transpose(banks[k][0:experts, t * P:(t + 1) * P], coef[:, t, :], ident[:, :]),
                              waits=[f["coef"], f["bank"][k]], signal=s_pe if t == blocks - 1 else None)

            def copy_step():
                f["coef_t"] = f["bank"][k] = act.add(lambda e: e.activation(coef_t[0:experts, :], banks[k][0:experts, :], ACT.Copy),
                                                     waits=[done, f["free"]], signal=s_act)
            put_off(1, copy_step)

        def down_bias(pair, k):
            for j in range(2):
                t = 2 * pair + j
                done = pe.add(lambda e, t=t, j=j: e.matmul(banks[k][:, j * width:(j + 1) * width], coef_t[0:experts, t * P:(t + 1) * P],
                                                           down_b[0:experts, :], start=True, stop=True),
                              waits=[f["coef_t"], f["bank"][k]], signal=s_pe if j else None)
            rows = slice(2 * pair, 2 * pair + 2)
            f["ffn", pair] = f["bank"][k] = dve.add(lambda e: e.tensor_tensor(
                ffn[:, rows, :], banks[k].rearrange("p (t c) -> p t c", t=2), x1_routed[:, rows, :], ALU.add),
                waits=[done, state["x1_routed"], f["free"]], signal=s_dve)

        def up_step(ex, fb, two):
            k = (GATE, UP)[two]
            i = (halves * ex + fb) % 2
            n = halves * ex + fb
            w = up_w[ex % 2]
            for c in range(halves):
                done = pe.add(lambda e, c=c: e.matmul(banks[k], w[:, c, 2 * P * fb + two:2 * P * (fb + 1):2], x1_t[:, c, :],
                                                      start=(c == 0), stop=(c == halves - 1)),
                              waits=[f["up_w", ex], f["x1_t"], f["bank"][k]], signal=s_pe if c == halves - 1 else None)
            if (fb, two) == (halves - 1, 1) and ex + 2 < experts:
                put_off(1, lambda: load_up(ex + 2, done))
            bias = up_b[:, (two * experts + ex) * halves + fb:(two * experts + ex) * halves + fb + 1]
            old = f.get(("inner", n - 2))
            if two == 0:
                gated = f["bank"][k] = dve.add(lambda e: e.tensor_scalar(gate[i], banks[k], bias, LIMIT, ALU.add, ALU.min),
                                               waits=[done, f["up_b"], old], signal=s_dve)

                def exp_step():
                    f["exp", n] = act.add(lambda e: e.activation(sigm[i], gate[i], ACT.Exp, scale=-SWIGLU_ALPHA),
                                          waits=[gated, old], signal=s_act)
                put_off(1, exp_step)
                return
            lifted = f["bank"][k] = dve.add(lambda e: e.tensor_scalar(lift[i], banks[k], bias, LIMIT, ALU.add, ALU.min),
                                            waits=[done, f["up_b"], old], signal=s_dve)
            lifted = dve.add(lambda e: e.tensor_scalar(lift[i], lift[i], -LIMIT, 1.0, ALU.max, ALU.add),
                             waits=[lifted], signal=s_dve)
            m = {}

            def sigmoid_steps():
                s = dve.add(lambda e: e.tensor_scalar(sigm[i], sigm[i], HUGE, 1.0, ALU.min, ALU.add),
                            waits=[f["exp", n]], signal=s_dve)
                m["more"] = s

            def invert_steps():
                s = act.add(lambda e: e.activation(sigm[i], sigm[i], ACT.Ln), waits=[m["more"]], signal=s_act)
                m["s"] = act.add(lambda e: e.activation(sigm[i], sigm[i], ACT.Exp, scale=-1.0), waits=[s], signal=s_act)

            def glu_step():
                m["glu"] = pool.add(lambda e: e.tensor_tensor(sigm[i], gate[i], sigm[i], ALU.mult), waits=[m["s"]], signal=s_pool)

            def inner_step():
                f["inner", n] = dve.add(lambda e: e.tensor_tensor(inner[ex % 2][:, fb, :], lift[i], sigm[i], ALU.mult),
                                        waits=[m["glu"], lifted, f.get(("down_read", ex - 2))], signal=s_dve)
            put_off(1, sigmoid_steps)
            put_off(2, invert_steps)
            put_off(2, glu_step)
            put_off(3, inner_step)

        def down_step(ex, pair):
            k = DOWN
            for j in range(2):
                t = 2 * pair + j
                for c in range(halves):
                    done = pe.add(lambda e, t=t, j=j, c=c: e.matmul(
                        banks[k][:, j * width:(j + 1) * width], inner[ex % 2][:, c, t * P:(t + 1) * P],
                        down_w[ex % 2][:, c, :], start=(c == 0), stop=(c == halves - 1)),
                        waits=[f["inner", halves * ex + halves - 1], f["down_w", ex], f["bank"][k]],
                        signal=s_pe if (j, c) == (1, halves - 1) else None)
            if pair == 1:
                f["down_read", ex] = done
                if ex + 2 < experts:
                    put_off(1, lambda: load_down(ex + 2, done))
            for j in range(2):
                t = 2 * pair + j
                summed = dve.add(lambda e, t=t, j=j: e.scalar_tensor_tensor(
                    out=ffn[:, t, :], in0=banks[k][:, j * width:(j + 1) * width],
                    scalar=coef[:, t, ex:ex + 1], in1=ffn[:, t, :], op0=ALU.mult, op1=ALU.add),
                    waits=[done, f["ffn", pair]], signal=s_dve)
            f["bank"][k] = f["ffn", pair] = summed

        def store_routed(done):
            sp.add(lambda e: e.dma_start(out[0].rearrange("(t p) c -> p t c", p=P), x1_t.rearrange("p h (t c) -> p (h t) c", c=width)),
                   waits=[done], signal=s_out, by=16)

        ffn_steps = [ffn_loads, None, lambda: transpose_x1(0, GATE), lambda: transpose_x1(1, UP),
                     lambda: transpose_up_bias(DOWN), None, lambda: transpose_coef(GATE), None,
                     lambda: down_bias(0, UP), lambda: down_bias(1, DOWN)]
        for ex in range(experts + 1):
            ups = [(lambda ex=ex, fb=fb, two=two: up_step(ex, fb, two)) if ex < experts else None
                   for fb in range(halves) for two in range(2)]
            downs = [(lambda ex=ex, fb=fb: down_step(ex - 1, fb)) if ex else None for fb in range(halves)]
            ffn_steps += ups[0:3] + downs[0:1] + ups[3:4] + downs[1:2]
        ffn_steps.reverse()

        act.add(lambda e: e.preload_act_table_set("natural_log_exp_and_others") or None)
        load_x(0)
        load_x(1)
        for unit in range(-UNITS - 2, end_of_units + UNITS):
            for slot in range(SLOTS):
                if 0 <= unit < end_of_units:
                    key_bank(unit, slot)
                if 0 <= unit + LEAD < end_of_units:
                    max_bank(unit + LEAD, slot)
                state["now"] = SLOTS * unit + slot
                weigh_slot(slot, unit)
                if slot == FINISH and 0 <= unit - 1 < end_of_units:
                    finish_unit(unit - 1)
                extra(unit, slot)
                turn_of_ffn = slot % FFN_TAIL_STEP == 0 if unit >= end_of_units else unit >= ffn_first and slot in FFN_SLOTS
                if turn_of_ffn and ffn_steps:
                    step = ffn_steps.pop()
                    if step:
                        step()
                run_put_off(state["now"])
        assert not ffn_steps
        while later:
            state["now"] = min(later)
            run_put_off(state["now"])
        layer_norm(x1_t.rearrange("p h (t c) -> p (h t) c", c=width), ffn, lambda: f["ffn", 1], store_routed)
        while later:
            state["now"] = min(later)
            run_put_off(state["now"])

        block = ctx.enter_context(nc.Block())

        @block.sync
        def _(engine):
            sp.run(engine)
            engine.wait_ge(s_out.semaphore, s_out.count)

        @block.gpsimd
        def _(engine):
            pool.run(engine)

        @block.scalar
        def _(engine):
            act.run(engine)

        @block.tensor
        def _(engine):
            pe.run(engine)

        @block.vector
        def _(engine):
            dve.run(engine)


NAMES = ["L0_attn_x", "L0_attn_W_attn", "L0_attn_b_attn", "L0_attn_W_k2", "L0_attn_b_k2", "L0_attn_W_proj",
         "L0_attn_b_proj", "L0_ffn_router_indices", "L0_ffn_routing_weights", "L0_ffn_gate_up_proj",
         "L0_ffn_gate_up_proj_bias", "L0_ffn_down_proj", "L0_ffn_down_proj_bias"]


def kernel(**inputs):
    import concourse.bacc as bacc
    from concourse.bass_utils import run_bass_kernel_spmd

    nc = bacc.Bacc("TRN2", target_bir_lowering=False, num_devices=1)
    arrays, args = {}, []
    for name in NAMES:
        a = np.ascontiguousarray(inputs[name])
        arrays[name] = a
        args.append(nc.dram_tensor(name, a.shape, mybir.dt.from_np(a.dtype), kind="ExternalInput").ap())
    shape = arrays["L0_attn_x"].shape
    args.append(nc.dram_tensor("layer_out", shape, F32, kind="ExternalOutput").ap())
    build_layer(nc, *args)
    result = run_bass_kernel_spmd(nc, [arrays], core_ids=[0])
    return result.results[0]["layer_out"]
```
